# Optimizing a Trainium2 kernel written in Bass

```python
import numpy as np
import jax
import jax.numpy as jnp

def _softmax(x, axis=-1):
    return jax.nn.softmax(x, axis=axis)

def _gelu(x):
    return jax.nn.gelu(x, approximate=True)

def _silu(x):
    return jax.nn.silu(x)

def _sigmoid(x):
    return jax.nn.sigmoid(x)

def _layernorm(x, axis=-1, eps=1e-05):
    m = jnp.mean(x, axis=axis, keepdims=True)
    v = jnp.var(x, axis=axis, keepdims=True)
    return (x - m) / jnp.sqrt(v + eps)

def _scatter_add(tgt, idx, src, axis=0):
    return tgt.at[idx].add(src)

def _segment_sum(src, seg, n):
    return jax.ops.segment_sum(src, seg, n)
kernel_name = 'mk_adaln_d2_jaxref_r8_508d01'

def setup_inputs(seed: int=0):
    np.random.seed(seed)
    _w = jnp.asarray

    def _L0_attn_setup():
        import jax, jax.numpy as jnp
        import numpy as np
        import math
        B, S, HID, H = (2, 256, 128, 16)
        D = HID // H

        def _get_slopes(n):
            start = 2 ** (-2 ** (-(math.log2(n) - 3)))
            return np.array([start * 2 ** (-i) for i in range(n)], dtype=np.float32)
        key = jax.random.key(seed)
        ks = jax.random.split(key, 9)
        sc = 1.0 / math.sqrt(HID)
        return {'x': jax.random.normal(ks[0], (B, S, HID), dtype=jnp.float32), 'Wq': jax.random.normal(ks[1], (HID, HID), dtype=jnp.float32) * sc, 'bq': jnp.zeros((HID,), dtype=jnp.float32), 'Wk': jax.random.normal(ks[2], (HID, HID), dtype=jnp.float32) * sc, 'bk': jnp.zeros((HID,), dtype=jnp.float32), 'Wv': jax.random.normal(ks[3], (HID, HID), dtype=jnp.float32) * sc, 'bv': jnp.zeros((HID,), dtype=jnp.float32), 'Wo': jax.random.normal(ks[4], (HID, HID), dtype=jnp.float32) * sc, 'bo': jnp.zeros((HID,), dtype=jnp.float32), 'slopes': jnp.asarray(_get_slopes(H))}
    _L0_attn_in = _L0_attn_setup()

    def _L0_ffn_setup():
        import jax, jax.numpy as jnp
        import numpy as np
        B, S, H = (4, 256, 128)
        E, K, INTER = (16, 2, 64)
        ALPHA, LIMIT = (1.702, 7.0)
        key = jax.random.key(seed)
        ks = jax.random.split(key, 6)
        return {'hidden_states': jax.random.normal(ks[0], (B, S, H), jnp.float32), 'router_weight': jax.random.normal(ks[1], (H, E), jnp.float32) * 0.02, 'gate_up_proj': jax.random.normal(ks[2], (E, H, 2 * INTER), jnp.float32) * 0.02, 'gate_up_proj_bias': jax.random.normal(ks[3], (E, 2 * INTER), jnp.float32) * 0.02, 'down_proj': jax.random.normal(ks[4], (E, INTER, H), jnp.float32) * 0.02, 'down_proj_bias': jax.random.normal(ks[5], (E, H), jnp.float32) * 0.02}
    _L0_ffn_in = _L0_ffn_setup()
    _L0_c = _w((lambda *s: np.random.randn(*s).astype(np.float32) * 0.05)(32, 128))
    _L0_wmod = _w((lambda *s: np.random.randn(*s).astype(np.float32) * 0.05)(128, 6 * 128) * 128 ** (-0.5))

    def _L1_attn_setup():
        import jax, jax.numpy as jnp
        import numpy as np
        N_HEADS = 16
        INPUT_DIM = 128
        EMBED_DIM = 128
        KEY_DIM = EMBED_DIM // N_HEADS
        BATCH = 4
        SEQ = 256

        def _uniform(key, shape, bound):
            return jax.random.uniform(key, shape, jnp.float32, -bound, bound)
        key = jax.random.key(seed)
        kq, k1, k2, k3, k4 = jax.random.split(key, 5)
        stdv_k = 1.0 / np.sqrt(KEY_DIM)
        stdv_e = 1.0 / np.sqrt(EMBED_DIM)
        return {'q': jax.random.normal(kq, (BATCH, SEQ, INPUT_DIM), jnp.float32), 'W_query': _uniform(k1, (N_HEADS, INPUT_DIM, KEY_DIM), stdv_k), 'W_key': _uniform(k2, (N_HEADS, INPUT_DIM, KEY_DIM), stdv_k), 'W_val': _uniform(k3, (N_HEADS, INPUT_DIM, KEY_DIM), stdv_k), 'W_out': _uniform(k4, (N_HEADS, KEY_DIM, EMBED_DIM), stdv_e)}
    _L1_attn_in = _L1_attn_setup()

    def _L1_ffn_setup():
        import jax, jax.numpy as jnp
        import numpy as np
        B, S, D = (4, 256, 128)
        E = 16
        K = 2
        F = 64
        FS = 256
        key = jax.random.key(seed)
        ks = jax.random.split(key, 9)
        s = 0.02
        return {'hidden_states': jax.random.normal(ks[0], (B, S, D), jnp.float32), 'router_w': jax.random.normal(ks[1], (E, D), jnp.float32) * s, 'Wg': jax.random.normal(ks[2], (E, D, F), jnp.float32) * s, 'Wu': jax.random.normal(ks[3], (E, D, F), jnp.float32) * s, 'Wd': jax.random.normal(ks[4], (E, F, D), jnp.float32) * s, 'Sg': jax.random.normal(ks[5], (D, FS), jnp.float32) * s, 'Su': jax.random.normal(ks[6], (D, FS), jnp.float32) * s, 'Sd': jax.random.normal(ks[7], (FS, D), jnp.float32) * s, 'shared_gate_w': jax.random.normal(ks[8], (D, 1), jnp.float32) * s}
    _L1_ffn_in = _L1_ffn_setup()
    _L1_c = _w((lambda *s: np.random.randn(*s).astype(np.float32) * 0.05)(32, 128))
    _L1_wmod = _w((lambda *s: np.random.randn(*s).astype(np.float32) * 0.05)(128, 6 * 128) * 128 ** (-0.5))
    _d = {'L0_attn_x': _L0_attn_in['x'], 'L0_attn_Wq': _L0_attn_in['Wq'], 'L0_attn_bq': _L0_attn_in['bq'], 'L0_attn_Wk': _L0_attn_in['Wk'], 'L0_attn_bk': _L0_attn_in['bk'], 'L0_attn_Wv': _L0_attn_in['Wv'], 'L0_attn_bv': _L0_attn_in['bv'], 'L0_attn_Wo': _L0_attn_in['Wo'], 'L0_attn_bo': _L0_attn_in['bo'], 'L0_attn_slopes': _L0_attn_in['slopes'], 'L0_ffn_router_weight': _L0_ffn_in['router_weight'], 'L0_ffn_gate_up_proj': _L0_ffn_in['gate_up_proj'], 'L0_ffn_gate_up_proj_bias': _L0_ffn_in['gate_up_proj_bias'], 'L0_ffn_down_proj': _L0_ffn_in['down_proj'], 'L0_ffn_down_proj_bias': _L0_ffn_in['down_proj_bias'], 'L0_c': _L0_c, 'L0_wmod': _L0_wmod, 'L1_attn_W_query': _L1_attn_in['W_query'], 'L1_attn_W_key': _L1_attn_in['W_key'], 'L1_attn_W_val': _L1_attn_in['W_val'], 'L1_attn_W_out': _L1_attn_in['W_out'], 'L1_ffn_router_w': _L1_ffn_in['router_w'], 'L1_ffn_Wg': _L1_ffn_in['Wg'], 'L1_ffn_Wu': _L1_ffn_in['Wu'], 'L1_ffn_Wd': _L1_ffn_in['Wd'], 'L1_ffn_Sg': _L1_ffn_in['Sg'], 'L1_ffn_Su': _L1_ffn_in['Su'], 'L1_ffn_Sd': _L1_ffn_in['Sd'], 'L1_ffn_shared_gate_w': _L1_ffn_in['shared_gate_w'], 'L1_c': _L1_c, 'L1_wmod': _L1_wmod}
    _x0 = _d['L0_attn_x']
    _d['L0_attn_x'] = jax.random.normal(jax.random.fold_in(jax.random.key(seed), 1), (32, 256, 128), dtype=_x0.dtype)
    del _x0
    return _d

def reference(L0_attn_x, L0_attn_Wq, L0_attn_bq, L0_attn_Wk, L0_attn_bk, L0_attn_Wv, L0_attn_bv, L0_attn_Wo, L0_attn_bo, L0_attn_slopes, L0_ffn_router_weight, L0_ffn_gate_up_proj, L0_ffn_gate_up_proj_bias, L0_ffn_down_proj, L0_ffn_down_proj_bias, L0_c, L0_wmod, L1_attn_W_query, L1_attn_W_key, L1_attn_W_val, L1_attn_W_out, L1_ffn_router_w, L1_ffn_Wg, L1_ffn_Wu, L1_ffn_Wd, L1_ffn_Sg, L1_ffn_Su, L1_ffn_Sd, L1_ffn_shared_gate_w, L1_c, L1_wmod):

    def _L0_attn_ref(x, Wq, bq, Wk, bk, Wv, bv, Wo, bo, slopes):
        import jax, jax.numpy as jnp
        import numpy as np
        import math
        B, S, HID, H = (2, 256, 128, 16)
        D = HID // H

        def _get_slopes(n):
            start = 2 ** (-2 ** (-(math.log2(n) - 3)))
            return np.array([start * 2 ** (-i) for i in range(n)], dtype=np.float32)
        b, s, hid = x.shape
        h = slopes.shape[0]
        d = hid // h
        q = (x @ Wq.T + bq).reshape(b, s, h, d).transpose(0, 2, 1, 3)
        k = (x @ Wk.T + bk).reshape(b, s, h, d).transpose(0, 2, 1, 3)
        v = (x @ Wv.T + bv).reshape(b, s, h, d).transpose(0, 2, 1, 3)
        scores = jnp.einsum('bhqd,bhkd->bhqk', q, k) / jnp.sqrt(jnp.float32(d))
        pos = jnp.arange(s)
        dist = (pos[None, :] - pos[:, None]).astype(x.dtype)
        scores = scores + slopes[None, :, None, None] * dist[None, None]
        attn = jax.nn.softmax(scores, axis=-1)
        ctx = jnp.einsum('bhqk,bhkd->bhqd', attn, v)
        ctx = ctx.transpose(0, 2, 1, 3).reshape(b, s, hid)
        return ctx @ Wo.T + bo

    def _L0_ffn_ref(hidden_states, router_weight, gate_up_proj, gate_up_proj_bias, down_proj, down_proj_bias):
        import jax, jax.numpy as jnp
        import numpy as np
        B, S, H = (4, 256, 128)
        E, K, INTER = (16, 2, 64)
        ALPHA, LIMIT = (1.702, 7.0)
        b, s, h = hidden_states.shape
        x = hidden_states.reshape(-1, h)
        logits = x @ router_weight
        topk_w, topk_i = jax.lax.top_k(logits, K)
        topk_w = jax.nn.softmax(topk_w, axis=-1)
        one_hot = (topk_i[..., None] == jnp.arange(E)[None, None, :]).astype(topk_w.dtype)
        scores = jnp.einsum('tk,tke->te', topk_w, one_hot)
        gu = jnp.einsum('th,ehf->tef', x, gate_up_proj) + gate_up_proj_bias
        gate = gu[..., ::2]
        up = gu[..., 1::2]
        gate = jnp.minimum(gate, LIMIT)
        up = jnp.clip(up, -LIMIT, LIMIT)
        glu = gate * jax.nn.sigmoid(gate * ALPHA)
        act = (up + 1.0) * glu
        out = jnp.einsum('tei,eih,te->th', act, down_proj, scores)
        out = out + jnp.einsum('te,eh->th', scores, down_proj_bias)
        return out.reshape(b, s, h)

    def _L1_attn_ref(q, W_query, W_key, W_val, W_out):
        import jax, jax.numpy as jnp
        import numpy as np
        N_HEADS = 16
        INPUT_DIM = 128
        EMBED_DIM = 128
        KEY_DIM = EMBED_DIM // N_HEADS
        BATCH = 4
        SEQ = 256

        def _uniform(key, shape, bound):
            return jax.random.uniform(key, shape, jnp.float32, -bound, bound)
        norm = 1.0 / np.sqrt(KEY_DIM)
        Q = jnp.einsum('bsd,hdk->hbsk', q, W_query)
        K = jnp.einsum('bsd,hdk->hbsk', q, W_key)
        V = jnp.einsum('bsd,hdv->hbsv', q, W_val)
        scores = norm * jnp.einsum('hbqk,hbnk->hbqn', Q, K)
        attn = jax.nn.softmax(scores, axis=-1)
        heads = jnp.einsum('hbqn,hbnv->hbqv', attn, V)
        out = jnp.einsum('hbqv,hve->bqe', heads, W_out)
        return out

    def _L1_ffn_ref(hidden_states, router_w, Wg, Wu, Wd, Sg, Su, Sd, shared_gate_w):
        import jax, jax.numpy as jnp
        import numpy as np
        B, S, D = (4, 256, 128)
        E = 16
        K = 2
        F = 64
        FS = 256
        b, s, d = hidden_states.shape
        x = hidden_states.reshape(-1, d)
        T = x.shape[0]
        logits = jnp.einsum('td,ed->te', x.astype(jnp.float32), router_w.astype(jnp.float32))
        probs = jax.nn.softmax(logits, axis=-1)
        top_w, top_i = jax.lax.top_k(probs, K)
        top_w = top_w / jnp.sum(top_w, axis=-1, keepdims=True)
        top_w = top_w.astype(x.dtype)
        dense_w = jnp.zeros((T, E), x.dtype).at[jnp.arange(T)[:, None], top_i].add(top_w)

        def body(acc, params):
            wg, wu, wd, cw = params
            h = jax.nn.silu(x @ wg) * (x @ wu)
            return (acc + cw[:, None] * (h @ wd), None)
        expert_out, _ = jax.lax.scan(body, jnp.zeros_like(x), (Wg, Wu, Wd, dense_w.T))
        shared = jax.nn.silu(x @ Sg) * (x @ Su) @ Sd
        shared = jax.nn.sigmoid(x @ shared_gate_w) * shared
        out = expert_out + shared
        return out.reshape(b, s, d)
    x = L0_attn_x
    mod = (_silu(L0_c) @ L0_wmod).reshape(L0_c.shape[0], 6, 1, -1)
    sa, ca, ga, sb, cb, gb = (mod[:, 0], mod[:, 1], mod[:, 2], mod[:, 3], mod[:, 4], mod[:, 5])
    ga = (2 * (ga >= 0) - 1) * jnp.maximum(jnp.abs(ga), 0.25)
    gb = (2 * (gb >= 0) - 1) * jnp.maximum(jnp.abs(gb), 0.25)
    h = _layernorm(x, axis=-1) * (1 + ca) + sa
    x = x + ga * _L0_attn_ref(h, L0_attn_Wq, L0_attn_bq, L0_attn_Wk, L0_attn_bk, L0_attn_Wv, L0_attn_bv, L0_attn_Wo, L0_attn_bo, L0_attn_slopes)
    h = _layernorm(x, axis=-1) * (1 + cb) + sb
    x = x + gb * _L0_ffn_ref(h, L0_ffn_router_weight, L0_ffn_gate_up_proj, L0_ffn_gate_up_proj_bias, L0_ffn_down_proj, L0_ffn_down_proj_bias)
    mod = (_silu(L1_c) @ L1_wmod).reshape(L1_c.shape[0], 6, 1, -1)
    sa, ca, ga, sb, cb, gb = (mod[:, 0], mod[:, 1], mod[:, 2], mod[:, 3], mod[:, 4], mod[:, 5])
    ga = (2 * (ga >= 0) - 1) * jnp.maximum(jnp.abs(ga), 0.25)
    gb = (2 * (gb >= 0) - 1) * jnp.maximum(jnp.abs(gb), 0.25)
    h = _layernorm(x, axis=-1) * (1 + ca) + sa
    x = x + ga * _L1_attn_ref(h, L1_attn_W_query, L1_attn_W_key, L1_attn_W_val, L1_attn_W_out)
    h = _layernorm(x, axis=-1) * (1 + cb) + sb
    x = x + gb * _L1_ffn_ref(h, L1_ffn_router_w, L1_ffn_Wg, L1_ffn_Wu, L1_ffn_Wd, L1_ffn_Sg, L1_ffn_Su, L1_ffn_Sd, L1_ffn_shared_gate_w)
    return x

_drawn_inputs = setup_inputs


def setup_inputs(seed=0):
    import zlib

    import numpy as np

    out = dict(_drawn_inputs(seed))
    spreads = {'L0_attn_bq': (0.0, 0.8),
     'L0_attn_bk': (0.0, 0.8),
     'L0_attn_bv': (0.0, 0.303),
     'L0_attn_bo': (0.0, 0.284)}
    factors = {'L0_ffn_router_weight': 8.0,
     'L0_ffn_gate_up_proj': 8.0,
     'L0_ffn_gate_up_proj_bias': 8.0,
     'L0_ffn_down_proj': 8.0,
     'L0_ffn_down_proj_bias': 8.0,
     'L1_ffn_router_w': 8.0,
     'L1_ffn_Wg': 8.0,
     'L1_ffn_Wu': 8.0,
     'L1_ffn_Wd': 8.0,
     'L1_ffn_Sg': 8.0,
     'L1_ffn_Su': 8.0,
     'L1_ffn_Sd': 8.0,
     'L1_ffn_shared_gate_w': 8.0}
    for name, (base, spread) in spreads.items():
        noise = np.random.default_rng([zlib.crc32(name.encode()), seed]).standard_normal(out[name].shape)
        drawn = base * np.exp(spread * noise) if base else spread * noise
        out[name] = jnp.asarray(drawn.astype(out[name].dtype))
    for name, factor in factors.items():
        out[name] = (out[name] * factor).astype(out[name].dtype)
    return out
```

```python
from contextlib import ExitStack

import numpy as np

import concourse.bass as bass
from concourse import mybir

F32 = mybir.dt.float32
BF16 = mybir.dt.bfloat16
U32 = mybir.dt.uint32
ALU = mybir.AluOpType
ACT = mybir.ActivationFunctionType
AX_X = mybir.AxisListType.X

P = 128
B = 32
S = 256
TT = S // P
D = 128
H = 16
DH = D // H
E = 16
F = 64
FS = 256
NJ = 6
R_PROD = NJ * DH
R_BIAS = R_PROD + 3
R_MAX = R_BIAS + 3
EC = 8
CW = EC * F
NQ = TT * E // EC
UNITS = 2 * B
LAGS = 6
SCALE = float(DH) ** -0.5
EPS = 1e-5
ALPHA, LIMIT = 1.702, 7.0
VW = 32

CHUNK_STEP = [0, 3, 8, 11]
SHARED_STEP = [6, 14]


def apart(eng, ready, value):
    if isinstance(value, int):
        return value
    value = eng.to_reg(value)
    eng.wait_ge(ready, 1)
    return value


class Unit:

    def __init__(self, j, first, lag):
        self.live = 0 <= first - lag < UNITS
        self.first = first - lag
        self.layer = 0 if self.first < B else 1
        self.no = j * 2 + self.first if self.live else None
        self.pair = j + self.first // 2 if self.live else None
        self.par = self.first % 2
        self.batch = self.no - B * self.layer if self.live else None

    def count(self, per, c):
        return self.no * per + c

    def count1(self, per, c):
        return (self.no - B) * per + c

    def count_pair(self, per):
        return self.pair * per + per

    def has(self, back):
        return self.first >= back


def iterations(eng):
    for base in (0, B):
        for n in range(base, base + LAGS):
            yield [Unit(0, n, lag) for lag in range(LAGS)]
        with eng.Fori(0, (B - LAGS) // 2) as j:
            for p in range(2):
                n0 = base + LAGS + p
                yield [Unit(j, n0, lag) for lag in range(LAGS)]
    for n in range(UNITS, UNITS + LAGS - 1):
        yield [Unit(0, n, lag) for lag in range(LAGS)]


JOBS = [
    ("act_t3", 5, (0, 1), 0), ("h_t", 0, (0, 1), 0), ("max_t1", 2, (0, 1), 1), ("qk", 0, (0, 1), 1),
    ("o_t0", 3, (0, 1), 0), ("sh_t1", 5, (1,), 1), ("o_t1", 3, (0, 1), 0), ("down1", 5, (0, 1), 1),
    ("v", 1, (0, 1), 0), ("act_t0", 4, (0, 1), 1), ("ctx_t", 3, (0, 1), 0), ("score_t", 4, (0,), 1),
    ("act_t1", 4, (0, 1), 0), ("wo", 3, (0, 1), 1), ("max_t0", 1, (0, 1), 0), ("sh_t0", 4, (1,), 1),
    ("down0", 4, (0, 1), 0), ("act_t2", 4, (0, 1), 1), ("h2_t", 3, (0, 1), 0), ("router", 3, (0, 1), 1),
]
BANK = {job: bank for job, _, _, bank in JOBS}


def build(nc, io, out):
    with ExitStack() as ctx:
        def sb(name, shape, dt=F32):
            return ctx.enter_context(nc.sbuf_tensor(name, shape, dt))

        def sem(name):
            return ctx.enter_context(nc.semaphore(name))

        def bank(name):
            return ctx.enter_context(nc.psum_tensor(name, [P, 512], F32))

        ps_s = bank("ps_s")
        ps_st = [bank("ps_st0"), bank("ps_st1")]
        ps_o = bank("ps_o")
        ps_g = bank("ps_g")
        ps_u = bank("ps_u")
        ps_job = [bank("ps_job0"), bank("ps_job1")]

        x = sb("x", [P, B, TT, D])
        ident = sb("ident", [P, P])
        ident_b = sb("ident_b", [P, P], BF16)
        ones_b = sb("ones_b", [P, P], BF16)
        ones_row = sb("ones_row", [1, P])
        neg_half = sb("neg_half", [P, TT])
        iota_e = sb("iota_e", [P, E])
        wq = [sb(f"wq{l}", [P, D]) for l in range(2)]
        wk = [sb(f"wk{l}", [P, D]) for l in range(2)]
        wv = [sb(f"wv{l}", [P, D]) for l in range(2)]
        wo = [sb(f"wo{l}", [P, D]) for l in range(2)]
        wr = [sb("wr0", [P, E]), sb("wr1", [P, E + 1])]
        wgu = [sb(f"wgu{l}", [P, 2, E * F]) for l in range(2)]
        wd = [sb(f"wd{l}", [P, E // 2, D]) for l in range(2)]
        wsgu = sb("wsgu", [P, 2, FS])
        wsd = sb("wsd", [P, FS // P, D])
        bq = sb("bq", [P, 1])
        bq_s = sb("bq_s", [P, 1])
        bk = sb("bk", [P, 1])
        bv = sb("bv", [P, 1])
        bo = sb("bo", [1, D])
        bo_v = sb("bo_v", [1, D])
        bd = sb("bd", [E, D])
        bd2 = sb("bd2", [E, D])
        c_t = [sb(f"c_t{l}", [P, B]) for l in range(2)]
        c_th = [sb(f"c_th{l}", [P, B]) for l in range(2)]
        c_si2 = [sb(f"c_si2{l}", [P, B]) for l in range(2)]
        c_si = [sb(f"c_si{l}", [P, B]) for l in range(2)]
        wmod = [sb(f"wmod{l}", [P, 6 * D]) for l in range(2)]
        mod = [sb(f"mod{l}", [P, 4, B]) for l in range(2)]
        g_up, g_down, g_pos, g_neg = ([sb(f"{n}{l}", [B, 2 * D]) for l in range(2)]
                                      for n in ("g_up", "g_down", "g_pos", "g_neg"))
        g_row = [sb(f"g_row{l}", [B, 2 * D]) for l in range(2)]
        b_in = sb("b_in", [2 * E, F])
        b_part = sb("b_part", [2 * E, 3, F], BF16)
        b_rest = sb("b_rest", [2 * E, 2, F])
        b_stack = sb("b_stack", [P, 2 * E * F], BF16)
        slopes = sb("slopes", [H, 1])
        pos = sb("pos", [H, S])
        ali = sb("ali", [H, S])
        ali_rest = sb("ali_rest", [H, 2, S])
        ali_part = sb("ali_part", [H, 3, S], BF16)

        ln_st = [sb(f"ln_st{i}", [P, TT, 6]) for i in range(2)]
        ln_mv = [sb(f"ln_mv{i}", [P, TT, 2]) for i in range(2)]
        ln_ve = [sb(f"ln_ve{i}", [P, TT]) for i in range(2)]
        ln_rs = [sb(f"ln_rs{i}", [P, TT]) for i in range(2)]
        xn = [sb(f"xn{i}", [P, TT, D]) for i in range(2)]
        h_t = [sb(f"h_t{i}", [P, S]) for i in range(2)]
        qk_f = sb("qk_f", [P, 2 * S])
        qk_rest = sb("qk_rest", [P, 2 * S])
        qk_part = sb("qk_part", [P, 3, 2 * S], BF16)
        q_stk = [sb(f"q_stk{i}", [P, H // 2, S], BF16) for i in range(2)]
        k_stk = [[sb(f"k_stk{l}{i}", [P, H // 2, S], BF16) for i in range(2)] for l in range(2)]
        v_ext = [sb(f"v_ext{i}", [P, TT, H, VW]) for i in range(2)]
        mx = sb("mx", [P, 2, TT, H // 2])
        mx_rest = sb("mx_rest", [P, 2, TT, H // 2])
        mx_part = [sb(f"mx_part{i}", [P, TT, 3, H // 2], BF16) for i in range(2)]
        mx_t = [sb(f"mx_t{i}", [3 * H // 2, S], BF16) for i in range(2)]
        prob = sb("prob", [P, 8, 2 * S])
        o_sb = sb("o_sb", [P, H // 4, S])
        den_r = sb("den_r", [P, TT, H])
        ctx_sb = sb("ctx_sb", [P, TT, D])
        ctx_t = sb("ctx_t", [P, S])
        att_tmp = sb("att_tmp", [P, TT, D])
        gate_a = [sb(f"gate_a{i}", [P, D]) for i in range(2)]
        gate_b = [sb(f"gate_b{i}", [P, D]) for i in range(2)]
        h2_t = [sb(f"h2_t{i}", [P, S]) for i in range(2)]
        lg = sb("lg", [P, TT, E + 1])
        top8 = sb("top8", [P, TT, 8])
        idx8 = sb("idx8", [P, TT, 8], U32)
        idx_f = sb("idx_f", [P, TT, 2])
        dz = sb("dz", [P, 2, TT])
        dz_th = sb("dz_th", [P, 2, TT])
        w_top = sb("w_top", [P, 2, TT])
        sh_gate = sb("sh_gate", [P, TT])
        hot1 = sb("hot1", [P, TT, E])
        hot2 = sb("hot2", [P, TT, E])
        score = sb("score", [P, TT, E])
        score_t = sb("score_t", [E, S])
        g_sb = sb("g_sb", [P, CW])
        th_sb = sb("th_sb", [P, CW])
        u_sb = sb("u_sb", [P, CW])
        glu_sb = sb("glu_sb", [P, CW])
        act_sb = sb("act_sb", [P, CW])
        act_w = [sb(f"act_w{i}", [P, CW]) for i in range(2)]
        act_t = [sb(f"act_t{i}", [P, CW // P, P]) for i in range(NQ)]
        sh_th = sb("sh_th", [P, FS])
        sh_glu = sb("sh_glu", [P, FS])
        sh_act = sb("sh_act", [P, FS])
        sh_t = [sb(f"sh_t{i}", [P, FS // P, P]) for i in range(TT)]
        ffn_tmp = sb("ffn_tmp", [P, TT, D])

        def dram(name, shape, dt):
            return nc.dram_tensor(name, shape, dt, kind="Internal").ap()

        gate_dram = [dram(f"gate_dram{l}", (B, 2 * D), F32) for l in range(2)]
        bias_dram = dram("bias_dram", (2 * E, 3, F), BF16)
        ali_dram = dram("ali_dram", (H, 3, S), BF16)
        part_dram = [dram(f"part_dram{i}", (2, P, NJ, S), BF16) for i in range(2)]
        max_dram = [dram(f"max_dram{i}", (3, 2, H // 4, S), BF16) for i in range(2)]

        first_loaded, x_first, rest_loaded, x_rest = sem("first_loaded"), sem("x_first"), sem("rest_loaded"), sem("x_rest")
        pool_const = sem("pool_const")
        pool_mask = sem("pool_mask")
        dve_const = sem("dve_const")
        c_tanh = sem("c_tanh")
        c_silu = sem("c_silu")
        mod_mm, mod_ok = sem("mod_mm"), sem("mod_ok")
        gate_ok, gate_stored = sem("gate_ok"), sem("gate_stored")
        bias_ok, bias_stored, bias_back = sem("bias_ok"), sem("bias_stored"), sem("bias_back")
        ali_ok, ali_stored, ali_back = sem("ali_ok"), sem("ali_stored"), sem("ali_back")
        bov_mm, bov_ok = sem("bov_mm"), sem("bov_ok")

        ln_done = [sem("ln1_done"), sem("ln2_done")]
        ln_rstd = [sem("ln1_rstd"), sem("ln2_rstd")]
        h_mm, h_ok = sem("h_mm"), sem("h_ok")
        qk_mm, qk_ok = sem("qk_mm"), sem("qk_ok")
        qk_hi, qk_r, qk_mid, qk_lo = sem("qk_hi"), sem("qk_r"), sem("qk_mid"), sem("qk_lo")
        parts_stored = sem("parts_stored")
        stk_loaded = [sem("stk_loaded0"), sem("stk_loaded1")]
        v_mm, v_ok = sem("v_mm"), sem("v_ok")
        s_mm, max_done = sem("s_mm"), sem("max_done")
        mx_split = sem("mx_split")
        mxt_mm, mxt_ok = sem("mxt_mm"), sem("mxt_ok")
        mx_stored = [sem("mx_stored0"), sem("mx_stored1")]
        mx_loaded = [sem("mx_loaded0"), sem("mx_loaded1")]
        st_mm, exp_done = sem("st_mm"), sem("exp_done")
        av_mm, o_ok = sem("av_mm"), sem("o_ok")
        ot_mm, ctx_norm = sem("ot_mm"), sem("ctx_norm")
        ctx_mm, ctx_ok = sem("ctx_mm"), sem("ctx_ok")
        wo_mm, att_scaled, att_added = sem("wo_mm"), sem("att_scaled"), sem("att_added")
        gate_a_in, gate_b_in = ([sem(f"{n}{i}") for i in range(2)] for n in ("gate_a_in", "gate_b_in"))
        h2_mm, h2_ok, rt_mm = sem("h2_mm"), sem("h2_ok"), sem("rt_mm")
        top_step = sem("top_step")
        z_ok, sg_ok = sem("z_ok"), sem("sg_ok")
        top_tanh = sem("top_tanh")
        score_step = sem("score_step")
        sct_mm, sct_ok = sem("sct_mm"), sem("sct_ok")
        g_mm, u_mm, th_ok = sem("g_mm"), sem("u_mm"), sem("th_ok")
        g_clip, u_clip = sem("g_clip"), sem("u_clip")
        glu_ok, act_ok, actw_ok = sem("glu_ok"), sem("act_ok"), sem("actw_ok")
        at_mm, at_ok = sem("at_mm"), sem("at_ok")
        sh_mm, sh_th_ok, sh_glu_ok, sh_act_ok = sem("sh_mm"), sem("sh_th_ok"), sem("sh_glu_ok"), sem("sh_act_ok")
        sht_mm, sht_ok = sem("sht_mm"), sem("sht_ok")
        dn_mm, ffn_scaled, ffn_added = sem("dn_mm"), sem("ffn_scaled"), sem("ffn_added")
        out_stored = sem("out_stored")

        TAKEN = {
            "act_t0": (at_ok, 4, 1), "act_t1": (at_ok, 4, 2), "act_t2": (at_ok, 4, 3), "act_t3": (at_ok, 4, 4),
            "max_t0": (mxt_ok, 2, 1), "max_t1": (mxt_ok, 2, 2), "h_t": (h_ok, 1, 1), "qk": (qk_ok, 2, 2),
            "o_t0": (ctx_norm, 4, 2), "o_t1": (ctx_norm, 4, 4), "down0": (ffn_scaled, 2, 1), "down1": (ffn_scaled, 2, 2),
            "v": (v_ok, 1, 1), "ctx_t": (ctx_ok, 1, 1), "score_t": (sct_ok, 1, 1), "wo": (att_scaled, 1, 1),
            "h2_t": (h2_ok, 1, 1), "router": (top_step, 9, 1), "sh_t0": (sht_ok, 2, 1), "sh_t1": (sht_ok, 2, 2),
        }

        FIRST_LOADS = 9
        REST_LOADS = 19
        GATE_STEPS = 5
        SPLIT_B = 8

        block = ctx.enter_context(nc.Block())

        @block.sync
        def _(sp):
            sp.dma_start(c_t[0][:], io["c0"]).then_inc(first_loaded, 16)
            sp.dma_start(wmod[0][:], io["wmod0"]).then_inc(first_loaded, 16)
            x_dram = io["x"].rearrange("b (t p) d -> p b t d", p=P)
            for t in range(TT):
                sp.dma_start(x[:, 0:SPLIT_B, t, :], x_dram[:, 0:SPLIT_B, t, :]).then_inc(x_first, 16)
            for dst, name in ((wq[0], "wq0"), (wk[0], "wk0"), (wv[0], "wv0"), (wo[0], "wo0"), (bq, "bq"), (bk, "bk"),
                              (slopes, "slopes")):
                sp.dma_start(dst[:], io[name]).then_inc(first_loaded, 16)
            for dst, name in ((b_in, "b_gu"), (bv, "bv"), (bo, "bo"), (bd, "bd"), (wr[0], "wr0"), (wgu[0], "wgu0"),
                              (wd[0], "wd0"), (c_t[1], "c1"), (wmod[1], "wmod1"), (wq[1], "wq1"), (wk[1], "wk1"),
                              (wv[1], "wv1"), (wo[1], "wo1"), (wgu[1], "wgu1"), (wd[1], "wd1"), (wsgu, "wsgu"),
                              (wsd, "wsd")):
                sp.dma_start(dst[:], io[name]).then_inc(rest_loaded, 16)
            sp.dma_start(wr[1][:, 0:E], io["wr1"]).then_inc(rest_loaded, 16)
            sp.dma_start(wr[1][:, E:E + 1], io["wsg"]).then_inc(rest_loaded, 16)
            sp.wait_ge(ali_ok, 6)
            sp.dma_start(ali_dram, ali_part[:]).then_inc(ali_stored, 16)
            sp.wait_ge(ali_stored, 16)
            sp.wait_ge(pool_const, 1)
            ali_rows = ali_dram.rearrange("(h par) j t -> par j h t", par=2)
            for i in range(2):
                for par in range(2):
                    r0 = 64 * par + R_PROD
                    sp.dma_start(k_stk[0][i][r0:r0 + 3], ali_rows[par]).then_inc(ali_back, 16)
            sp.wait_ge(gate_ok, GATE_STEPS)
            sp.dma_start(gate_dram[0], g_row[0][:]).then_inc(gate_stored, 16)
            sp.wait_ge(bias_ok, 5)
            sp.dma_start(bias_dram, b_part[:]).then_inc(bias_stored, 16)
            for t in range(TT):
                sp.dma_start(x[:, SPLIT_B:B, t, :], x_dram[:, SPLIT_B:B, t, :]).then_inc(x_rest, 16)
            sp.wait_ge(bias_stored, 16)
            sp.dma_start(b_stack[0:3, :].rearrange("j (e f) -> j e f", f=F),
                         bias_dram.rearrange("e j f -> j e f")).then_inc(bias_back, 16)
            sp.wait_ge(gate_ok, 2 * GATE_STEPS)
            sp.dma_start(gate_dram[1], g_row[1][:]).then_inc(gate_stored, 16)
            sp.wait_ge(gate_stored, 32)

            def max_rows(u, half):
                ready = apart(sp, pool_const, u.count(2, 1 + half))
                sp.wait_ge(mxt_ok, ready)
                if u.has(1):
                    ready = apart(sp, pool_const, u.count(32, 0))
                    sp.wait_ge(mx_loaded[half], ready)
                sp.dma_start(max_dram[half].rearrange("j par h t -> (j par h) t"), mx_t[half][:])\
                  .then_inc(mx_stored[half], 16)
                ready = apart(sp, pool_const, u.count(16, 16))
                sp.wait_ge(mx_stored[half], ready)
                for par in range(2):
                    r0 = 64 * par + R_BIAS
                    sp.dma_start(q_stk[u.par][r0:r0 + 3, half * 4:half * 4 + 4, :], max_dram[half][:, par])\
                      .then_inc(mx_loaded[half], 16)

            def stack_rows(u, half):
                for qk in range(2):
                    dst = (q_stk[u.par], k_stk[u.layer][u.par])[qk]
                    src = part_dram[u.par][qk].rearrange("(h par d) j t -> par (d j) h t", par=2, d=DH)
                    for par in range(2):
                        sp.dma_start(dst[64 * par:64 * par + R_PROD, half * 4:half * 4 + 4, :],
                                     src[par, :, half * 4:half * 4 + 4, :]).then_inc(stk_loaded[half], 16)

            for u0, u1, u2, u3, u4, u5 in iterations(sp):
                if u2.live:
                    if u2.has(2):
                        ready = apart(sp, pool_const, u2.count(1, -1))
                        sp.wait_ge(att_scaled, ready)
                    sp.dma_start(gate_a[u2.par][:], gate_dram[u2.layer][bass.ds(u2.batch, 1), 0:D].broadcast_to([P, D]))\
                      .then_inc(gate_a_in[u2.par], 16)
                    max_rows(u2, 1)
                if u3.live:
                    if u3.has(2):
                        ready = apart(sp, pool_const, u3.count(2, -2))
                        sp.wait_ge(ffn_scaled, ready)
                    sp.dma_start(gate_b[u3.par][:], gate_dram[u3.layer][bass.ds(u3.batch, 1), D:2 * D].broadcast_to([P, D]))\
                      .then_inc(gate_b_in[u3.par], 16)
                if u5.live and u5.layer == 1:
                    ready = apart(sp, pool_const, u5.count(2, 2))
                    sp.wait_ge(ffn_added, ready)
                    sp.dma_start(out[bass.ds(u5.batch, 1)].rearrange("b (t p) d -> p (b t) d", p=P),
                                 x[:, bass.ds(u5.batch, 1), :, :].rearrange("p b t d -> p (b t) d")).then_inc(out_stored, 16)
                if u0.live:
                    ready = apart(sp, pool_const, u0.count(1, 1))
                    sp.wait_ge(qk_lo, ready)
                    if u0.has(2):
                        for half in range(2):
                            ready = apart(sp, pool_const, u0.count(64, -64))
                            sp.wait_ge(stk_loaded[half], ready)
                    dst = part_dram[u0.par]
                    for j0, nj, part in ((0, 3, 0), (3, 2, 1), (5, 1, 2)):
                        sp.dma_start(dst[0, :, j0:j0 + nj, :],
                                     qk_part[:, part:part + 1, 0:S].broadcast_to([P, nj, S])).then_inc(parts_stored, 16)
                    for j0, nj in ((0, 3), (3, 2), (5, 1)):
                        sp.dma_start(dst[1, :, j0:j0 + nj, :], qk_part[:, 0:nj, S:2 * S]).then_inc(parts_stored, 16)
                    ready = apart(sp, pool_const, u0.count(96, 96))
                    sp.wait_ge(parts_stored, ready)
                    if u0.has(2):
                        ready = apart(sp, pool_const, u0.count(16, -32 + 8))
                        sp.wait_ge(st_mm, ready)
                    stack_rows(u0, 0)
                if u1.live:
                    max_rows(u1, 0)
                if u0.live:
                    if u0.has(2):
                        ready = apart(sp, pool_const, u0.count(16, -16))
                        sp.wait_ge(st_mm, ready)
                    stack_rows(u0, 1)
            sp.wait_ge(out_stored, 16 * B)

        @block.gpsimd
        def _(pool):
            pool.wait_ge(dve_const, 1)
            pool.affine_select(out=ident[:], in_=ident[:], compare_op=ALU.not_equal, fill=1.0, base=0,
                               pattern=[[-1, P]], channel_multiplier=1).then_inc(pool_mask, 1)
            masks = 1
            for k2 in k_stk:
                for k in k2:
                    for r in (32, 96):
                        pool.wait_ge(pool_mask, masks)
                        pool.affine_select(out=k[r:r + 32], in_=k[r:r + 32], compare_op=ALU.is_ge, fill=0.0,
                                           base=-(R_BIAS - 32), pattern=[[0, H // 2], [0, S]],
                                           channel_multiplier=1).then_inc(pool_mask, 1)
                        masks += 1
            pool.wait_ge(pool_mask, masks)
            pool.iota(pos[:], [[1, S]], base=-(S - 1), channel_multiplier=0, allow_small_or_imprecise_dtypes=True)\
                .then_inc(pool_const, 1)
            pool.iota(iota_e[:], [[1, E]], base=0, channel_multiplier=0, allow_small_or_imprecise_dtypes=True)\
                .then_inc(pool_const, 1)

            def rstd(u, i):
                ready = apart(pool, dve_const, u.count(6, 4))
                pool.wait_ge(ln_done[i], ready)
                pool.tensor_scalar(ln_ve[i][:], ln_mv[i][:, :, 1], EPS, None, ALU.add).then_inc(ln_rstd[i], 1)
                pool.wait_ge(ln_rstd[i], u.count(2, 1))
                pool.tensor_tensor(ln_rs[i][:], ln_ve[i][:], neg_half[:], ALU.pow).then_inc(ln_rstd[i], 1)

            def weigh(u, q):
                t, e0 = q // 2, (q % 2) * EC
                pool.wait_ge(act_ok, u.count(4, q + 1))
                if q == 0:
                    pool.wait_ge(score_step, u.count(5, 5))
                if u.has(1) or q >= 2:
                    pool.wait_ge(at_mm, u.count(4, q - 1))
                pool.tensor_tensor(act_w[q % 2][:].rearrange("p (e f) -> p e f", f=F),
                                   act_sb[:].rearrange("p (e f) -> p e f", f=F),
                                   score[:, t, e0:e0 + EC].rearrange("p (e o) -> p e o", o=1).broadcast_to([P, EC, F]),
                                   ALU.mult).then_inc(actw_ok, 1)

            for u0, u1, u2, u3, u4, u5 in iterations(pool):
                if u0.live:
                    rstd(u0, 0)
                if u4.live:
                    ready = apart(pool, dve_const, u4.count(9, 9))
                    pool.wait_ge(top_step, ready)
                    if u4.layer == 0 and u4.has(1):
                        pool.wait_ge(sct_mm, u4.count(1, 0))
                    for t in range(TT):
                        for k, hot in ((0, hot1), (1, hot2)):
                            pool.tensor_scalar(hot[:, t, :], iota_e[:], idx_f[:, t, k:k + 1], w_top[:, k, t:t + 1],
                                               ALU.is_equal, ALU.mult).then_inc(score_step, 1)
                    pool.wait_ge(score_step, u4.count(5, 4))
                    pool.tensor_tensor(score[:], hot1[:], hot2[:], ALU.add).then_inc(score_step, 1)
                    weigh(u4, 0)
                if u5.live:
                    ready = apart(pool, dve_const, u5.count(2, 2))
                    pool.wait_ge(ffn_scaled, ready)
                    xt = x[:, bass.ds(u5.batch, 1), 1, :]
                    pool.tensor_tensor(xt, xt, ffn_tmp[:, 1:2, :], ALU.add).then_inc(ffn_added, 1)
                if u0.live:
                    pool.wait_ge(qk_hi, u0.count(1, 1))
                    pool.tensor_tensor(qk_rest[:], qk_f[:], qk_part[:, 0, :], ALU.subtract).then_inc(qk_r, 1)
                    pool.wait_ge(qk_mid, u0.count(1, 1))
                    pool.tensor_tensor(qk_part[:, 2, :], qk_rest[:], qk_part[:, 1, :], ALU.subtract).then_inc(qk_lo, 1)
                if u4.live:
                    weigh(u4, 1)
                if u3.live:
                    ready = apart(pool, dve_const, u3.count(1, 1))
                    pool.wait_ge(att_scaled, ready)
                    xt = x[:, bass.ds(u3.batch, 1), :, :].rearrange("p b t d -> p (b t) d")
                    pool.tensor_tensor(xt, xt, att_tmp[:], ALU.add).then_inc(att_added, 1)
                    rstd(u3, 1)
                if u4.live:
                    weigh(u4, 2)
                    ready = apart(pool, dve_const, u4.count(2, 1))
                    pool.wait_ge(ffn_scaled, ready)
                    xt = x[:, bass.ds(u4.batch, 1), 0, :]
                    pool.tensor_tensor(xt, xt, ffn_tmp[:, 0:1, :], ALU.add).then_inc(ffn_added, 1)
                    weigh(u4, 3)

        @block.scalar
        def _(act):
            act.wait_ge(first_loaded, 16 * FIRST_LOADS)
            act.activation(c_th[0][:], c_t[0][:], ACT.Tanh, scale=0.5).then_inc(c_tanh, 1)
            act.activation(bq_s[:], bq[:], ACT.Copy, scale=SCALE).then_inc(c_tanh, 1)
            act.wait_ge(rest_loaded, 16 * REST_LOADS)
            act.activation(c_th[1][:], c_t[1][:], ACT.Tanh, scale=0.5).then_inc(c_tanh, 1)
            act.wait_ge(c_tanh, 2)
            act.wait_ge(mod_ok, 2)

            def tanh_top(u):
                act.wait_ge(top_step, u.count(9, 7))
                if u.layer == 1:
                    act.wait_ge(z_ok, u.count1(1, 1))
                n = 1 + u.layer
                act.activation(dz_th[:, 0:n, :], dz[:, 0:n, :], ACT.Tanh, scale=0.5).then_inc(top_tanh, 1)

            def tanh_gate(u, q):
                if u.layer == 0:
                    act.wait_ge(g_clip, u.count(4, q + 1))
                else:
                    act.wait_ge(g_mm, u.count(4, q + 1))
                if u.has(1) or q:
                    act.wait_ge(glu_ok, u.count(4, q))
                if u.layer == 0:
                    act.activation(th_sb[:], g_sb[:], ACT.Tanh, scale=0.5 * ALPHA).then_inc(th_ok, 1)
                else:
                    act.activation(th_sb[:], ps_g[:], ACT.Tanh, scale=0.5).then_inc(th_ok, 1)

            def tanh_shared(u, t):
                if u.layer == 1:
                    act.wait_ge(sh_mm, u.count1(2, t + 1))
                    act.activation(sh_th[:], ps_g[:, 0:FS], ACT.Tanh, scale=0.5).then_inc(sh_th_ok, 1)

            def take_act_t(u, q):
                act.wait_ge(at_mm, u.count(4, q + 1))
                act.activation(act_t[q][:].rearrange("p a b -> p (a b)"), ps_job[BANK[f"act_t{q}"]][:], ACT.Copy)\
                   .then_inc(at_ok, 1)

            def take_sh_t(u, t):
                if u.layer == 1:
                    act.wait_ge(sht_mm, u.count1(2, t + 1))
                    act.activation(sh_t[t][:].rearrange("p a b -> p (a b)"), ps_job[BANK[f"sh_t{t}"]][:, 0:FS], ACT.Copy)\
                       .then_inc(sht_ok, 1)

            def take_max_t(u, half):
                act.wait_ge(mxt_mm, u.count(2, half + 1))
                if u.has(1):
                    act.wait_ge(mx_stored[half], u.count(16, 0))
                act.activation(mx_t[half][:], ps_job[BANK[f"max_t{half}"]][:].bitcast(BF16)[0:3 * H // 2, 0:S], ACT.Copy)\
                   .then_inc(mxt_ok, 1)

            def take_h(u, i, mm, ok, dst, job):
                act.wait_ge(mm, u.count(1, 1))
                act.activation(dst[u.par][:], ps_job[BANK[job]][:, 0:S], ACT.Identity,
                               scale=mod[u.layer][:, 2 * i + 1, bass.ds(u.batch, 1)],
                               bias=mod[u.layer][:, 2 * i, bass.ds(u.batch, 1)]).then_inc(ok, 1)

            def take_o(u, phase):
                act.wait_ge(av_mm, u.count(4, 2 * phase + 2))
                if phase == 0 and u.has(1):
                    act.wait_ge(ot_mm, u.count(2, 0))
                act.activation(o_sb[:, 2 * phase:2 * phase + 2, :].rearrange("p g s -> p (g s)"), ps_o[:], ACT.Copy)\
                   .then_inc(o_ok, 1)

            def take_qk(u):
                act.wait_ge(qk_mm, u.count(1, 1))
                if u.has(1):
                    act.wait_ge(qk_r, u.count(1, 0))
                b = ps_job[BANK["qk"]]
                if u.layer == 0:
                    act.activation(qk_f[:, 0:S], b[:, 0:S], ACT.Identity, scale=SCALE, bias=bq_s[:]).then_inc(qk_ok, 1)
                    act.activation(qk_f[:, S:2 * S], b[:, S:2 * S], ACT.Identity, bias=bk[:]).then_inc(qk_ok, 1)
                else:
                    act.activation(qk_f[:, 0:S], b[:, 0:S], ACT.Copy, scale=SCALE).then_inc(qk_ok, 1)
                    act.activation(qk_f[:, S:2 * S], b[:, S:2 * S], ACT.Copy).then_inc(qk_ok, 1)

            for u0, u1, u2, u3, u4, u5 in iterations(act):
                if u0.live and u0.first == B:
                    act.wait_ge(mod_ok, 4)
                for k in range(H):
                    if u2.live:
                        act.wait_ge(st_mm, u2.count(16, k + 1))
                        if k >= 8:
                            act.wait_ge(av_mm, u2.count(4, (k - 8) // 4 + 1))
                        elif u2.has(1):
                            act.wait_ge(av_mm, u2.count(4, (k + 8) // 4 - 3))
                        act.activation(prob[:, k % 8, :], ps_st[k % 2][:], ACT.Exp).then_inc(exp_done, 1)
                    if k == 0 and u5.live:
                        take_act_t(u5, 3)
                    if k == 1 and u4.live:
                        tanh_gate(u4, 0)
                    if k == 2:
                        if u3.live:
                            take_o(u3, 1)
                        if u4.live:
                            tanh_top(u4)
                        if u0.live:
                            take_h(u0, 0, h_mm, h_ok, h_t, "h_t")
                        if u2.live:
                            take_max_t(u2, 1)
                    if k == 3 and u0.live:
                        take_qk(u0)
                    if k == 4:
                        if u5.live:
                            take_sh_t(u5, 1)
                        if u0.live:
                            act.wait_ge(qk_ok, u0.count(2, 2))
                            if u0.has(1):
                                act.wait_ge(parts_stored, u0.count(96, 0))
                            act.activation(qk_part[:, 0, :], qk_f[:], ACT.Copy).then_inc(qk_hi, 1)
                        if u4.live:
                            tanh_gate(u4, 1)
                    if k == 6:
                        if u1.live:
                            act.wait_ge(v_mm, u1.count(1, 1))
                            act.activation(v_ext[u1.par][:, :, :, 0:DH],
                                           ps_job[BANK["v"]][:, 0:S].rearrange("p (t h d) -> p t h d", t=TT, h=H),
                                           ACT.Copy).then_inc(v_ok, 1)
                        if u0.live:
                            act.wait_ge(qk_r, u0.count(1, 1))
                            act.activation(qk_part[:, 1, :], qk_rest[:], ACT.Copy).then_inc(qk_mid, 1)
                    if k == 7:
                        if u4.live:
                            take_act_t(u4, 0)
                        if u3.live:
                            act.wait_ge(ctx_mm, u3.count(1, 1))
                            act.activation(ctx_t[:], ps_job[BANK["ctx_t"]][:, 0:S], ACT.Copy).then_inc(ctx_ok, 1)
                        if u4.live:
                            tanh_shared(u4, 0)
                    if k == 8 and u4.live:
                        if u4.layer == 0:
                            act.wait_ge(sct_mm, u4.count(1, 1))
                            act.activation(score_t[:], ps_job[BANK["score_t"]][0:E, 0:S], ACT.Copy).then_inc(sct_ok, 1)
                        take_act_t(u4, 1)
                    if k == 9 and u4.live:
                        tanh_gate(u4, 2)
                    if k == 10:
                        if u2.live:
                            take_o(u2, 0)
                        if u1.live:
                            take_max_t(u1, 0)
                    if k == 11 and u4.live:
                        take_sh_t(u4, 0)
                    if k == 12 and u4.live:
                        tanh_gate(u4, 3)
                    if k == 13 and u4.live:
                        take_act_t(u4, 2)
                    if k == 14:
                        if u3.live:
                            take_h(u3, 1, h2_mm, h2_ok, h2_t, "h2_t")
                    if k == 15 and u4.live:
                        tanh_shared(u4, 1)

        @block.tensor
        def _(pe):
            pe.wait_ge(first_loaded, 16 * FIRST_LOADS)
            for l in range(2):
                pe.wait_ge(c_silu, 2 * l + 2)
                if l:
                    pe.wait_ge(rest_loaded, 16 * REST_LOADS)
                    pe.wait_ge(mod_ok, 2)
                    pe.wait_ge(gate_ok, GATE_STEPS)
                for i, ch in enumerate((0, 1, 3, 4)):
                    pe.matmul(ps_g[:, i * B:(i + 1) * B], wmod[l][:, ch * D:(ch + 1) * D], c_si[l][:],
                              start=True, stop=True)
                for i, ch in enumerate((2, 5)):
                    mm = pe.matmul(ps_u[0:B, i * D:(i + 1) * D], c_si[l][:], wmod[l][:, ch * D:(ch + 1) * D],
                                   start=True, stop=True)
                mm.then_inc(mod_mm, 1)
            pe.matmul(ps_s[0:1, 0:D], bv[:], wo[0][:], start=True, stop=True).then_inc(bov_mm, 1)
            pe.wait_ge(mod_ok, 4)
            pe.wait_ge(gate_ok, 2 * GATE_STEPS)
            pe.wait_ge(bov_ok, 1)
            pe.wait_ge(dve_const, 3)
            pe.wait_ge(pool_const, 1)
            pe.wait_ge(ali_back, 64)

            waited = {}

            def job(name):
                b = BANK[name]
                if b in waited:
                    s, value = waited[b]
                    pe.wait_ge(s, value)
                return ps_job[b]

            def issued(name, u):
                s, per, c = TAKEN[name]
                value = u.count1(per, c) if s is sht_ok else u.count(per, c)
                waited[BANK[name]] = (s, value)

            def chunk_gate(u, q):
                if q == 0:
                    pe.wait_ge(h2_ok, u.count(1, 1))
                if u.layer == 0:
                    if u.has(1) or q:
                        pe.wait_ge(g_clip, u.count(4, q))
                elif q in (0, 2):
                    if u.first == B:
                        pe.wait_ge(g_clip, 4 * B) if q == 0 else pe.wait_ge(sh_act_ok, u.count1(2, 1))
                    else:
                        pe.wait_ge(sh_act_ok, u.count1(2, q // 2))
                else:
                    pe.wait_ge(glu_ok, u.count(4, q))
                chunk(u, q, ps_g, 0).then_inc(g_mm, 1)

            def chunk_up(u, q):
                if u.layer == 0 or (u.first == B and q == 0):
                    if u.has(1) or q:
                        pe.wait_ge(u_clip, u.count(4, q))
                else:
                    pe.wait_ge(act_ok, u.count(4, q))
                chunk(u, q, ps_u, 1).then_inc(u_mm, 1)

            def chunk(u, q, dst, gu):
                t, c0 = q // 2, (q % 2) * CW
                if u.layer == 0:
                    pe.matmul(dst[:], ones_b[:], b_stack[:, gu * E * F + c0:gu * E * F + c0 + CW], start=True, stop=False)
                return pe.matmul(dst[:], h2_t[u.par][:, t * P:(t + 1) * P], wgu[u.layer][:, gu, c0:c0 + CW],
                                 start=u.layer == 1, stop=True)

            def shared(u, t):
                if u.layer == 1:
                    pe.wait_ge(glu_ok, u.count(4, 2 * t + 2))
                    for gu in range(2):
                        mm = pe.matmul(ps_g[:, gu * FS:(gu + 1) * FS], h2_t[u.par][:, t * P:(t + 1) * P],
                                       wsgu[:, gu, :], start=True, stop=True)
                    mm.then_inc(sh_mm, 1)

            def act_transpose(u, q):
                pe.wait_ge(actw_ok, u.count(4, q + 1))
                b = job(f"act_t{q}")
                for j in range(CW // P):
                    mm = pe.transpose(b[:, j * P:(j + 1) * P], act_w[q % 2][:, j * P:(j + 1) * P], ident[:])
                mm.then_inc(at_mm, 1)
                issued(f"act_t{q}", u)

            def sh_transpose(u, t):
                if u.layer == 1:
                    pe.wait_ge(sh_act_ok, u.count1(2, t + 1))
                    b = job(f"sh_t{t}")
                    for j in range(FS // P):
                        mm = pe.transpose(b[:, j * P:(j + 1) * P], sh_act[:, j * P:(j + 1) * P], ident[:])
                    mm.then_inc(sht_mm, 1)
                    issued(f"sh_t{t}", u)

            def down(u, t):
                pe.wait_ge(at_ok, u.count(4, 2 * t + 2))
                if u.layer == 0:
                    if t == 0:
                        pe.wait_ge(sct_ok, u.count(1, 1))
                else:
                    pe.wait_ge(sht_ok, u.count1(2, t + 1))
                b = job(f"down{t}")
                pairs = [(act_t[2 * t + j // 4][:, j % 4, :], wd[u.layer][:, j, :]) for j in range(E // 2)]
                if u.layer == 0:
                    pairs.append((score_t[:, t * P:(t + 1) * P], bd2[:]))
                else:
                    pairs += [(sh_t[t][:, j, :], wsd[:, j, :]) for j in range(FS // P)]
                for j, (lhs_t, rhs) in enumerate(pairs):
                    mm = pe.matmul(b[:, 0:D], lhs_t, rhs, start=j == 0, stop=j == len(pairs) - 1)
                mm.then_inc(dn_mm, 1)
                issued(f"down{t}", u)

            def max_transpose(u, half):
                pe.wait_ge(mx_split, u.count(8, 4 * half + 4))
                b = job(f"max_t{half}")
                for t in range(TT):
                    mm = pe.transpose(b[:].bitcast(BF16)[0:3 * H // 2, t * P:(t + 1) * P],
                                      mx_part[half][:, t].rearrange("p j h -> p (j h)"), ident_b[:])
                mm.then_inc(mxt_mm, 1)
                issued(f"max_t{half}", u)

            def probs_values(u, g):
                pe.wait_ge(exp_done, u.count(16, 4 * g + 4))
                if g == 0:
                    pe.wait_ge(v_ok, u.count(1, 1))
                if g % 2 == 0 and (u.has(1) or g):
                    pe.wait_ge(o_ok, u.count(2, g // 2))
                for kt in range(TT):
                    for i in range(4):
                        h = 4 * g + i
                        mm = pe.matmul(ps_o[32 * i:32 * i + 32, (g % 2) * S:(g % 2 + 1) * S], v_ext[u.par][:, kt, h, :],
                                       prob[:, h % 8, kt * S:(kt + 1) * S], start=g % 2 == 0 and kt == 0,
                                       stop=kt == TT - 1, skip_group_check=True)
                mm.then_inc(av_mm, 1)

            def out_transpose(u, t):
                if t == 0:
                    pe.wait_ge(o_ok, u.count(2, 2))
                b = job(f"o_t{t}")
                for g in range(H // 4):
                    mm = pe.transpose(b[:, g * P:(g + 1) * P], o_sb[:, g, t * P:(t + 1) * P], ident[:])
                mm.then_inc(ot_mm, 1)
                issued(f"o_t{t}", u)

            def norm_transpose(u, i, name, done):
                pe.wait_ge(ln_done[i], u.count(6, 6))
                b = job(name)
                for t in range(TT):
                    mm = pe.transpose(b[:, t * P:(t + 1) * P], xn[i][:, t, :], ident[:])
                mm.then_inc(done, 1)
                issued(name, u)

            for u0, u1, u2, u3, u4, u5 in iterations(pe):
                for k in range(H):
                    hp, par = k // 2, k % 2
                    r0 = 64 * par
                    if u1.live:
                        if k % 8 == 0:
                            pe.wait_ge(stk_loaded[k // 8], u1.count(64, 64))
                        if k or u1.has(1):
                            pe.wait_ge(max_done, u1.count(16, k))
                        q, kk = q_stk[u1.par], k_stk[u1.layer][u1.par]
                        for t in range(TT):
                            mm = pe.matmul(ps_s[:, t * S:(t + 1) * S], q[r0:r0 + R_BIAS, hp, t * P:(t + 1) * P],
                                           kk[r0:r0 + R_BIAS, hp, :], start=True, stop=True)
                        mm.then_inc(s_mm, 1)
                    if u2.live:
                        if k % 8 == 0:
                            pe.wait_ge(mx_loaded[k // 8], u2.count(32, 32))
                        if k >= 2 or u2.has(1):
                            pe.wait_ge(exp_done, u2.count(16, k - 1))
                        q, kk = q_stk[u2.par], k_stk[u2.layer][u2.par]
                        for t in range(TT):
                            mm = pe.matmul(ps_st[k % 2][:, t * S:(t + 1) * S], kk[r0:r0 + R_MAX, hp, t * P:(t + 1) * P],
                                           q[r0:r0 + R_MAX, hp, :], start=True, stop=True)
                        mm.then_inc(st_mm, 1)
                    if u4.live:
                        if u4.first == 0 and k == 0:
                            pe.wait_ge(bias_back, 16)
                            pe.wait_ge(dve_const, 4)
                        for q in range(NQ):
                            if k == CHUNK_STEP[q]:
                                chunk_gate(u4, q)
                            if k == CHUNK_STEP[q] + 1:
                                chunk_up(u4, q)
                        for t in range(TT):
                            if k == SHARED_STEP[t]:
                                shared(u4, t)
                    if k == 0 and u5.live:
                        act_transpose(u5, 3)
                    if k == 1 and u3.live:
                        probs_values(u3, 3)
                    if k == 2:
                        if u0.live:
                            norm_transpose(u0, 0, "h_t", h_mm)
                        if u2.live:
                            max_transpose(u2, 1)
                    if k == 3:
                        if u0.live:
                            pe.wait_ge(h_ok, u0.count(1, 1))
                            b = job("qk")
                            pe.matmul(b[:, 0:S], wq[u0.layer][:], h_t[u0.par][:], start=True, stop=True)
                            pe.matmul(b[:, S:2 * S], wk[u0.layer][:], h_t[u0.par][:], start=True, stop=True)\
                              .then_inc(qk_mm, 1)
                            issued("qk", u0)
                        if u3.live:
                            out_transpose(u3, 0)
                    if k == 4 and u5.live:
                        sh_transpose(u5, 1)
                    if k == 5:
                        if u3.live:
                            out_transpose(u3, 1)
                        if u5.live:
                            down(u5, 1)
                    if k in (5, 9, 13) and u2.live:
                        probs_values(u2, k // 4 - 1)
                    if k == 6 and u1.live:
                        b = job("v")
                        for t in range(TT):
                            mm = pe.matmul(b[:, t * D:(t + 1) * D], h_t[u1.par][:, t * P:(t + 1) * P],
                                           wv[u1.layer][:], start=True, stop=True)
                        mm.then_inc(v_mm, 1)
                        issued("v", u1)
                    if k == 7:
                        if u4.live:
                            act_transpose(u4, 0)
                        if u3.live:
                            pe.wait_ge(ctx_norm, u3.count(4, 4))
                            b = job("ctx_t")
                            for t in range(TT):
                                mm = pe.transpose(b[:, t * P:(t + 1) * P], ctx_sb[:, t, :], ident[:])
                            mm.then_inc(ctx_mm, 1)
                            issued("ctx_t", u3)
                    if k == 8 and u4.live:
                        if u4.layer == 0:
                            pe.wait_ge(score_step, u4.count(5, 5))
                            b = job("score_t")
                            for t in range(TT):
                                mm = pe.transpose(b[0:E, t * P:(t + 1) * P], score[:, t, :], ident[:])
                            mm.then_inc(sct_mm, 1)
                            issued("score_t", u4)
                        act_transpose(u4, 1)
                    if k == 9 and u3.live:
                        pe.wait_ge(ctx_ok, u3.count(1, 1))
                        b = job("wo")
                        for t in range(TT):
                            if u3.layer == 0:
                                pe.matmul(b[:, t * D:(t + 1) * D], ones_row[:], bo_v[:], start=True, stop=False)
                            mm = pe.matmul(b[:, t * D:(t + 1) * D], ctx_t[:, t * P:(t + 1) * P], wo[u3.layer][:],
                                           start=u3.layer == 1, stop=True)
                        mm.then_inc(wo_mm, 1)
                        issued("wo", u3)
                    if k == 10 and u1.live:
                        max_transpose(u1, 0)
                    if k == 11 and u4.live:
                        sh_transpose(u4, 0)
                    if k == 12 and u4.live:
                        down(u4, 0)
                    if k == 13 and u4.live:
                        act_transpose(u4, 2)
                    if k == 14 and u3.live:
                        norm_transpose(u3, 1, "h2_t", h2_mm)
                    if k == 15 and u3.live:
                        pe.wait_ge(h2_ok, u3.count(1, 1))
                        b = job("router")
                        n = E + u3.layer
                        for t in range(TT):
                            mm = pe.matmul(b[:, t * 32:t * 32 + n], h2_t[u3.par][:, t * P:(t + 1) * P], wr[u3.layer][:],
                                           start=True, stop=True)
                        mm.then_inc(rt_mm, 1)
                        issued("router", u3)

        @block.vector
        def _(dve):
            dve.memset(ident[:], 0.0)
            for k2 in k_stk:
                for k in k2:
                    for r in (32, 96):
                        last = dve.memset(k[r:r + 32], -1.0)
            last.then_inc(dve_const, 1)
            dve.memset(neg_half[:], -0.5)
            dve.memset(ones_b[:], 1.0)
            dve.memset(ones_row[:], 1.0)
            dve.memset(b_stack[:], 0.0)
            for v in v_ext:
                dve.memset(v[:, :, :, DH + 1:VW], 0.0)
                dve.memset(v[:, :, :, DH:DH + 1], 1.0)
            for q in q_stk:
                for r in (32, 96):
                    last = dve.memset(q[r:r + 32], 1.0)
            last.then_inc(dve_const, 1)
            dve.wait_ge(pool_const, 2)
            dve.tensor_copy(ident_b[:], ident[:]).then_inc(dve_const, 1)
            dve.wait_ge(first_loaded, 16 * FIRST_LOADS)

            def split(src, rest, part, done, c):
                dve.tensor_copy(part[:, 0], src).then_inc(done, 1)
                dve.wait_ge(done, c + 1)
                dve.tensor_tensor(rest[:, 0], src, part[:, 0], ALU.subtract).then_inc(done, 1)
                dve.wait_ge(done, c + 2)
                dve.tensor_copy(part[:, 1], rest[:, 0]).then_inc(done, 1)
                dve.wait_ge(done, c + 3)
                dve.tensor_tensor(rest[:, 1], rest[:, 0], part[:, 1], ALU.subtract).then_inc(done, 1)
                dve.wait_ge(done, c + 4)
                dve.tensor_copy(part[:, 2], rest[:, 1]).then_inc(done, 1)

            dve.tensor_scalar(ali[:], pos[:], slopes[:], None, ALU.mult).then_inc(ali_ok, 1)
            dve.wait_ge(ali_ok, 1)
            split(ali[:], ali_rest, ali_part, ali_ok, 1)

            def modulation(l):
                dve.wait_ge(c_tanh, 1 + 2 * l)
                dve.scalar_tensor_tensor(out=c_si2[l][:], in0=c_th[l][:], scalar=1.0, in1=c_t[l][:], op0=ALU.add,
                                         op1=ALU.mult).then_inc(c_silu, 1)
                dve.wait_ge(c_silu, 2 * l + 1)
                dve.tensor_scalar(c_si[l][:], c_si2[l][:], 0.5, None, ALU.mult).then_inc(c_silu, 1)
                dve.wait_ge(mod_mm, l + 1)
                m = ps_g[:, 0:4 * B].rearrange("p (a b) -> p a b", b=B)
                for i in range(2):
                    dve.tensor_scalar(mod[l][:, i::2, :], m[:, i::2, :], float(i), None, ALU.add).then_inc(mod_ok, 1)
                g = ps_u[0:B, 0:2 * D]
                dve.tensor_scalar(g_up[l][:], g, 0.25, None, ALU.max).then_inc(gate_ok, 1)
                dve.tensor_scalar(g_down[l][:], g, -0.25, None, ALU.min).then_inc(gate_ok, 1)
                dve.wait_ge(gate_ok, GATE_STEPS * l + 2)
                dve.scalar_tensor_tensor(out=g_pos[l][:], in0=g, scalar=0.0, in1=g_up[l][:], op0=ALU.is_ge,
                                         op1=ALU.mult).then_inc(gate_ok, 1)
                dve.scalar_tensor_tensor(out=g_neg[l][:], in0=g, scalar=0.0, in1=g_down[l][:], op0=ALU.is_lt,
                                         op1=ALU.mult).then_inc(gate_ok, 1)
                dve.wait_ge(gate_ok, GATE_STEPS * l + 4)
                dve.tensor_tensor(g_row[l][:], g_pos[l][:], g_neg[l][:], ALU.add).then_inc(gate_ok, 1)

            modulation(0)
            dve.wait_ge(rest_loaded, 16 * REST_LOADS)
            split(b_in[:], b_rest, b_part, bias_ok, 0)
            modulation(1)
            dve.wait_ge(bov_mm, 1)
            dve.tensor_tensor(bo_v[:], ps_s[0:1, 0:D], bo[:], ALU.add).then_inc(bov_ok, 1)
            dve.tensor_scalar(bd2[:], bd[:], 2.0, None, ALU.mult).then_inc(dve_const, 1)

            def norm_stats(u, i):
                for t in range(TT):
                    dve.bn_stats(ln_st[i][:, t, :], x[:, bass.ds(u.batch, 1), t, :].rearrange("p b d -> p (b d)"))\
                       .then_inc(ln_done[i], 1)
                ready = apart(dve, pool_const, u.count(6, 2))
                dve.wait_ge(ln_done[i], ready)
                for t in range(TT):
                    dve.bn_aggr(ln_mv[i][:, t, :], ln_st[i][:, t, :]).then_inc(ln_done[i], 1)

            def norm_apply(u, i, used):
                dve.wait_ge(ln_rstd[i], u.count(2, 2))
                if u.has(1):
                    dve.wait_ge(used, u.count(1, 0))
                for t in range(TT):
                    dve.tensor_scalar(xn[i][:, t:t + 1, :], x[:, bass.ds(u.batch, 1), t, :], ln_mv[i][:, t, 0:1],
                                      ln_rs[i][:, t:t + 1], ALU.subtract, ALU.mult).then_inc(ln_done[i], 1)

            def max_split(u, half):
                c = 4 * half
                dve.wait_ge(max_done, u.count(16, 8 * half + 8))
                if u.has(1):
                    dve.wait_ge(mxt_mm, u.count(2, half - 1))
                src, rest, part = mx[:, half], mx_rest[:, half], mx_part[half]
                dve.tensor_copy(part[:, :, 0, :], src).then_inc(mx_split, 1)
                dve.wait_ge(mx_split, u.count(8, c + 1))
                dve.tensor_tensor(rest, src, part[:, :, 0, :], ALU.subtract).then_inc(mx_split, 1)
                dve.wait_ge(mx_split, u.count(8, c + 2))
                dve.tensor_copy(part[:, :, 1, :], rest).then_inc(mx_split, 1)
                dve.wait_ge(mx_split, u.count(8, c + 3))
                dve.tensor_tensor(part[:, :, 2, :], rest, part[:, :, 1, :], ALU.subtract).then_inc(mx_split, 1)

            def clip_gate(u, q):
                if u.layer == 0:
                    dve.wait_ge(g_mm, u.count(4, q + 1))
                    if u.has(1) or q:
                        dve.wait_ge(th_ok, u.count(4, q))
                    dve.tensor_scalar(g_sb[:], ps_g[:], LIMIT, None, ALU.min).then_inc(g_clip, 1)

            def glu(u, q):
                if u.layer == 0:
                    dve.wait_ge(u_mm, u.count(4, q + 1))
                    dve.tensor_scalar(u_sb[:], ps_u[:], -LIMIT, LIMIT, ALU.max, ALU.min).then_inc(u_clip, 1)
                dve.wait_ge(th_ok, u.count(4, q + 1))
                dve.scalar_tensor_tensor(out=glu_sb[:], in0=th_sb[:], scalar=1.0, in1=g_sb[:] if u.layer == 0 else ps_g[:],
                                         op0=ALU.add, op1=ALU.mult).then_inc(glu_ok, 1)

            def expert_act(u, q):
                dve.wait_ge(glu_ok, u.count(4, q + 1))
                if u.has(1) or q:
                    dve.wait_ge(actw_ok, u.count(4, q))
                if u.layer == 0:
                    dve.wait_ge(u_clip, u.count(4, q + 1))
                    dve.scalar_tensor_tensor(out=act_sb[:], in0=u_sb[:], scalar=1.0, in1=glu_sb[:], op0=ALU.add,
                                             op1=ALU.mult).then_inc(act_ok, 1)
                else:
                    dve.wait_ge(u_mm, u.count(4, q + 1))
                    dve.tensor_tensor(act_sb[:], ps_u[:], glu_sb[:], ALU.mult).then_inc(act_ok, 1)

            def shared_act(u, t):
                if u.layer == 1:
                    dve.wait_ge(sh_th_ok, u.count1(2, t + 1))
                    dve.scalar_tensor_tensor(out=sh_glu[:], in0=sh_th[:], scalar=1.0, in1=ps_g[:, 0:FS], op0=ALU.add,
                                             op1=ALU.mult).then_inc(sh_glu_ok, 1)
                    dve.wait_ge(sh_glu_ok, u.count1(2, t + 1))
                    dve.wait_ge(sg_ok, u.count1(1, 1))
                    if u.first > B or t:
                        dve.wait_ge(sht_mm, u.count1(2, t))
                    dve.scalar_tensor_tensor(out=sh_act[:], in0=sh_glu[:], scalar=sh_gate[:, t:t + 1],
                                             in1=ps_g[:, FS:2 * FS], op0=ALU.mult, op1=ALU.mult).then_inc(sh_act_ok, 1)

            def normalise(u, t):
                dve.wait_ge(ot_mm, u.count(2, t + 1))
                o = ps_job[BANK[f"o_t{t}"]][:].rearrange("p (h v) -> p h v", v=VW)
                dve.reciprocal(den_r[:, t, :].rearrange("p (h o) -> p h o", o=1), o[:, :, DH:DH + 1]).then_inc(ctx_norm, 1)
                dve.wait_ge(ctx_norm, u.count(4, 2 * t + 1))
                if t == 0 and u.has(1):
                    dve.wait_ge(ctx_mm, u.count(1, 0))
                dve.tensor_tensor(ctx_sb[:, t, :].rearrange("p (h d) -> p h d", d=DH), o[:, :, 0:DH],
                                  den_r[:, t, :].rearrange("p (h o) -> p h o", o=1).broadcast_to([P, H, DH]), ALU.mult)\
                   .then_inc(ctx_norm, 1)

            def scale_ffn(u, t):
                dve.wait_ge(dn_mm, u.count(2, t + 1))
                dve.wait_ge(gate_b_in[u.par], u.count_pair(16))
                if u.has(1):
                    dve.wait_ge(ffn_added, u.count(2, t - 1))
                dve.tensor_tensor(ffn_tmp[:, t, :], ps_job[BANK[f"down{t}"]][:, 0:D], gate_b[u.par][:], ALU.mult)\
                   .then_inc(ffn_scaled, 1)

            def top_two(u):
                n = E + u.layer
                dve.wait_ge(rt_mm, u.count(1, 1))
                r = ps_job[BANK["router"]][:, 0:TT * 32].rearrange("p (t e) -> p t e", e=32)
                dve.tensor_copy(lg[:, :, 0:n], r[:, :, 0:n]).then_inc(top_step, 1)
                ready = apart(dve, pool_const, u.count(9, 1))
                dve.wait_ge(top_step, ready)
                for t in range(TT):
                    dve.max(top8[:, t, :], lg[:, t, 0:E]).then_inc(top_step, 1)
                if u.layer == 1:
                    dve.tensor_copy(dz[:, 1, :], lg[:, :, E]).then_inc(z_ok, 1)
                ready = apart(dve, pool_const, u.count(9, 3))
                dve.wait_ge(top_step, ready)
                for t in range(TT):
                    dve.max_index(idx8[:, t, :], top8[:, t, :], lg[:, t, 0:E]).then_inc(top_step, 1)
                dve.wait_ge(top_step, u.count(9, 5))
                if u.has(1):
                    dve.wait_ge(score_step, u.count(5, -1))
                dve.tensor_copy(idx_f[:], idx8[:, :, 0:2]).then_inc(top_step, 1)
                dve.tensor_tensor(dz[:, 0, :], top8[:, :, 0], top8[:, :, 1], ALU.subtract).then_inc(top_step, 1)

            def top_weights(u):
                dve.wait_ge(top_tanh, u.count(1, 1))
                for k, sign in ((0, 0.25), (1, -0.25)):
                    dve.tensor_scalar(w_top[:, k, :], dz_th[:, 0, :], sign, 0.25, ALU.mult, ALU.add).then_inc(top_step, 1)
                if u.layer == 1:
                    dve.tensor_scalar(sh_gate[:], dz_th[:, 1, :], 0.25, 0.25, ALU.mult, ALU.add).then_inc(sg_ok, 1)

            for u0, u1, u2, u3, u4, u5 in iterations(dve):
                if u0.first == 0:
                    dve.wait_ge(x_first, 16 * TT)
                if u0.first == LAGS - 1:
                    dve.wait_ge(x_rest, 16 * TT)
                for k in range(H):
                    if u1.live:
                        dve.wait_ge(s_mm, u1.count(16, k + 1))
                        hp, par = k // 2, k % 2
                        dve.tensor_reduce(mx[:, hp // 4, :, 4 * par + hp % 4],
                                          ps_s[:].rearrange("p (t s) -> p t s", s=S), AX_X, ALU.max).then_inc(max_done, 1)
                    if k == 0:
                        if u2.live:
                            max_split(u2, 1)
                        if u0.live:
                            if u0.layer == 1:
                                dve.wait_ge(ffn_added, u0.count(2, 2 - 2 * B))
                            norm_stats(u0, 0)
                    if k == 1 and u4.live:
                        clip_gate(u4, 0)
                        top_two(u4)
                    if k == 2:
                        if u0.live:
                            norm_apply(u0, 0, h_mm)
                        if u4.live:
                            glu(u4, 0)
                            top_weights(u4)
                    if k == 3 and u4.live:
                        expert_act(u4, 0)
                    if k == 4:
                        if u3.live:
                            normalise(u3, 0)
                        if u4.live:
                            clip_gate(u4, 1)
                    if k == 5:
                        if u3.live:
                            normalise(u3, 1)
                        if u4.live:
                            glu(u4, 1)
                    if k == 6:
                        if u5.live:
                            scale_ffn(u5, 1)
                        if u4.live:
                            expert_act(u4, 1)
                    if k == 7 and u4.live:
                        shared_act(u4, 0)
                    if k == 8 and u1.live:
                        max_split(u1, 0)
                    if k == 9 and u4.live:
                        clip_gate(u4, 2)
                    if k == 10:
                        if u3.live:
                            dve.wait_ge(wo_mm, u3.count(1, 1))
                            dve.wait_ge(gate_a_in[u3.par], u3.count_pair(16))
                            if u3.has(1):
                                dve.wait_ge(att_added, u3.count(1, 0))
                            dve.tensor_tensor(att_tmp[:], ps_job[BANK["wo"]][:, 0:TT * D].rearrange("p (t d) -> p t d", d=D),
                                              gate_a[u3.par][:].rearrange("p (o d) -> p o d", o=1).broadcast_to([P, TT, D]),
                                              ALU.mult).then_inc(att_scaled, 1)
                        if u4.live:
                            glu(u4, 2)
                    if k == 11:
                        if u4.live:
                            expert_act(u4, 2)
                        if u3.live:
                            dve.wait_ge(att_added, u3.count(1, 1))
                            norm_stats(u3, 1)
                    if k == 12:
                        if u4.live:
                            clip_gate(u4, 3)
                        if u3.live:
                            norm_apply(u3, 1, h2_mm)
                    if k == 13 and u4.live:
                        scale_ffn(u4, 0)
                        glu(u4, 3)
                    if k == 14 and u4.live:
                        expert_act(u4, 3)
                    if k == 15 and u4.live:
                        shared_act(u4, 1)


def kernel(**inputs):
    import concourse.bacc as bacc
    from concourse.bass_utils import run_bass_kernel_spmd

    a = {n: np.ascontiguousarray(v) for n, v in inputs.items()}
    gu0 = a["L0_ffn_gate_up_proj"].reshape(E, D, F, 2).transpose(1, 3, 0, 2).reshape(D, 2, E * F)
    heads = lambda w: w.transpose(1, 0, 2).reshape(D, D)
    arrays = {
        "x": a["L0_attn_x"],
        "c0": a["L0_c"].T, "c1": a["L1_c"].T, "wmod0": a["L0_wmod"], "wmod1": a["L1_wmod"],
        "wq0": a["L0_attn_Wq"].T, "wk0": a["L0_attn_Wk"].T, "wv0": a["L0_attn_Wv"].T, "wo0": a["L0_attn_Wo"].T,
        "bq": a["L0_attn_bq"].reshape(D, 1), "bk": a["L0_attn_bk"].reshape(D, 1), "bv": a["L0_attn_bv"].reshape(D, 1),
        "bo": a["L0_attn_bo"].reshape(1, D), "slopes": a["L0_attn_slopes"].reshape(H, 1),
        "wr0": a["L0_ffn_router_weight"], "wgu0": gu0,
        "b_gu": a["L0_ffn_gate_up_proj_bias"].reshape(E, F, 2).transpose(2, 0, 1).reshape(2 * E, F),
        "wd0": a["L0_ffn_down_proj"].reshape(E // 2, 2 * F, D).transpose(1, 0, 2), "bd": a["L0_ffn_down_proj_bias"],
        "wq1": heads(a["L1_attn_W_query"]), "wk1": heads(a["L1_attn_W_key"]), "wv1": heads(a["L1_attn_W_val"]),
        "wo1": a["L1_attn_W_out"].reshape(D, D), "wr1": a["L1_ffn_router_w"].T, "wsg": a["L1_ffn_shared_gate_w"],
        "wgu1": np.stack([a["L1_ffn_Wg"].transpose(1, 0, 2).reshape(D, E * F),
                          a["L1_ffn_Wu"].transpose(1, 0, 2).reshape(D, E * F)], axis=1),
        "wd1": a["L1_ffn_Wd"].reshape(E // 2, 2 * F, D).transpose(1, 0, 2),
        "wsgu": np.stack([a["L1_ffn_Sg"], a["L1_ffn_Su"]], axis=1),
        "wsd": a["L1_ffn_Sd"].reshape(FS // P, P, D).transpose(1, 0, 2),
    }
    nc = bacc.Bacc("TRN2", target_bir_lowering=False, num_devices=1)
    feeds, io = {}, {}
    for name, v in arrays.items():
        v = np.ascontiguousarray(v)
        feeds[f"in_{name}"] = v
        io[name] = nc.dram_tensor(f"in_{name}", v.shape, mybir.dt.from_np(v.dtype), kind="ExternalInput").ap()
    out = nc.dram_tensor("out_x", (B, S, D), F32, kind="ExternalOutput").ap()
    build(nc, io, out)
    r = run_bass_kernel_spmd(nc, [feeds], core_ids=[0])
    return r.results[0]["out_x"]
```

```python
from contextlib import ExitStack

import numpy as np

import concourse.bass as bass
from concourse import mybir

F32 = mybir.dt.float32
BF16 = mybir.dt.bfloat16
F32R = mybir.dt.float32r
U32 = mybir.dt.uint32
ALU = mybir.AluOpType
ACT = mybir.ActivationFunctionType
AX_X = mybir.AxisListType.X

P = 128
B = 32
S = 256
TT = S // P
D = 128
H = 16
DH = D // H
E = 16
F = 64
FS = 256
NJ = 6
R_PROD = NJ * DH
R_BIAS = R_PROD + 3
R_MAX = R_BIAS + 3
EC = 8
CW = EC * F
NQ = TT * E // EC
UNITS = 2 * B
LAGS = 6
SCALE = float(DH) ** -0.5
EPS = 1e-5
ALPHA, LIMIT = 1.702, 7.0
VW = 32

GATE_STEP = [[0, 3, 7, 11], [0, 3, 8, 11]]
UP_STEP = [2, 5, 10, 13]
SHARED_STEP = [6, 13]


def apart(eng, ready, value):
    if isinstance(value, int):
        return value
    value = eng.to_reg(value)
    eng.wait_ge(ready, 1)
    return value


class Unit:

    def __init__(self, j, first, lag):
        self.live = 0 <= first - lag < UNITS
        self.first = first - lag
        self.layer = 0 if self.first < B else 1
        self.no = j * 2 + self.first if self.live else None
        self.pair = j + self.first // 2 if self.live else None
        self.par = self.first % 2
        self.batch = self.no - B * self.layer if self.live else None

    def count(self, per, c):
        return self.no * per + c

    def count1(self, per, c):
        return (self.no - B) * per + c

    def count_pair(self, per):
        return self.pair * per + per

    def has(self, back):
        return self.first >= back


def iterations(eng):
    for base in (0, B):
        for n in range(base, base + LAGS):
            yield [Unit(0, n, lag) for lag in range(LAGS)]
        with eng.Fori(0, (B - LAGS) // 2) as j:
            for p in range(2):
                n0 = base + LAGS + p
                yield [Unit(j, n0, lag) for lag in range(LAGS)]
    for n in range(UNITS, UNITS + LAGS - 1):
        yield [Unit(0, n, lag) for lag in range(LAGS)]


JOBS = [
    ("act_t3", 5, (0, 1), 1), ("sh_t1", 5, (1,), 1), ("h_t", 0, (0, 1), 0), ("max_t1", 2, (0, 1), 1),
    ("o_t0", 3, (0, 1), 1), ("qk", 0, (0, 1), 0), ("o_t1", 3, (0, 1), 1), ("v", 1, (0, 1), 0),
    ("down1", 5, (0, 1), 0), ("ctx_t", 3, (0, 1), 1), ("act_t0", 4, (0, 1), 0), ("wo", 3, (0, 1), 1),
    ("score_t", 4, (0,), 0), ("max_t0", 1, (0, 1), 0), ("act_t1", 4, (0, 1), 1), ("sh_t0", 4, (1,), 0),
    ("down0", 4, (0, 1), 1), ("act_t2", 4, (0, 1), 0), ("h2_t", 3, (0, 1), 1), ("router", 3, (0, 1), 0),
]
BANK = {job: bank for job, _, _, bank in JOBS}


def build(nc, io, out):
    with ExitStack() as ctx:
        def sb(name, shape, dt=F32):
            return ctx.enter_context(nc.sbuf_tensor(name, shape, dt))

        def sem(name):
            return ctx.enter_context(nc.semaphore(name))

        def bank(name):
            return ctx.enter_context(nc.psum_tensor(name, [P, 512], F32))

        ps_s = bank("ps_s")
        ps_st = [bank("ps_st0"), bank("ps_st1")]
        ps_o = bank("ps_o")
        ps_g = bank("ps_g")
        ps_u = bank("ps_u")
        ps_job = [bank("ps_job0"), bank("ps_job1")]

        x = sb("x", [P, B, TT, D])
        ident = sb("ident", [P, P])
        ident_b = sb("ident_b", [P, P], BF16)
        ones_b = sb("ones_b", [P, P], BF16)
        ones_row = sb("ones_row", [1, P])
        neg_half = sb("neg_half", [P, TT])
        iota_e = sb("iota_e", [P, E])
        wq = [sb(f"wq{l}", [P, D]) for l in range(2)]
        wk = [sb(f"wk{l}", [P, D]) for l in range(2)]
        wv = [sb(f"wv{l}", [P, D]) for l in range(2)]
        wo = [sb(f"wo{l}", [P, D]) for l in range(2)]
        wr = [sb("wr0", [P, E]), sb("wr1", [P, E + 1])]
        wgu_hi = [sb(f"wgu_hi{l}", [P, 2, E * F], F32R) for l in range(2)]
        wgu_lo = [sb(f"wgu_lo{l}", [P, 2, E * F], F32R) for l in range(2)]
        wd = [sb(f"wd{l}", [P, E // 2, D]) for l in range(2)]
        wsgu_hi = sb("wsgu_hi", [P, 2, FS], F32R)
        wsgu_lo = sb("wsgu_lo", [P, 2, FS], F32R)
        wsd = sb("wsd", [P, FS // P, D])
        bq = sb("bq", [P, 1])
        bq_s = sb("bq_s", [P, 1])
        bk = sb("bk", [P, 1])
        bv = sb("bv", [P, 1])
        bo = sb("bo", [1, D])
        bo_v = sb("bo_v", [1, D])
        bd = sb("bd", [E, D])
        bd2 = sb("bd2", [E, D])
        c_t = [sb(f"c_t{l}", [P, B]) for l in range(2)]
        c_th = [sb(f"c_th{l}", [P, B]) for l in range(2)]
        c_si2 = [sb(f"c_si2{l}", [P, B]) for l in range(2)]
        c_si = [sb(f"c_si{l}", [P, B]) for l in range(2)]
        mod = [sb(f"mod{l}", [P, 4, B]) for l in range(2)]
        g_row = [sb(f"g_row{l}", [B, 2 * D]) for l in range(2)]
        b_in = sb("b_in", [E, 2, F])
        b_part = sb("b_part", [E, 3, 2 * F], BF16)
        b_rest = sb("b_rest", [E, 2, 2 * F])
        b_stack = sb("b_stack", [P, 2 * E * F], BF16)
        slopes = sb("slopes", [H, 1])
        pos = sb("pos", [H, S])
        ali = sb("ali", [H, S])
        ali_rest = sb("ali_rest", [H, 2, S])
        ali_part = sb("ali_part", [H, 3, S], BF16)

        ln_st = [sb(f"ln_st{i}", [P, TT, 6]) for i in range(2)]
        ln_mv = [sb(f"ln_mv{i}", [P, TT, 2]) for i in range(2)]
        ln_ve = [sb(f"ln_ve{i}", [P, TT]) for i in range(2)]
        ln_rs = [sb(f"ln_rs{i}", [P, TT]) for i in range(2)]
        xn = [sb(f"xn{i}", [P, TT, D]) for i in range(2)]
        h_t = [sb(f"h_t{i}", [P, S]) for i in range(2)]
        qk_f = sb("qk_f", [P, 2 * S])
        qk_rest = sb("qk_rest", [P, 2 * S])
        qk_part = sb("qk_part", [P, 3, 2 * S], BF16)
        q_stk = [sb(f"q_stk{i}", [P, H // 2, S], BF16) for i in range(2)]
        k_stk = [[sb(f"k_stk{l}{i}", [P, H // 2, S], BF16) for i in range(2)] for l in range(2)]
        v_ext = [sb(f"v_ext{i}", [P, TT, H, VW]) for i in range(2)]
        mx = sb("mx", [P, 2, TT, H // 2])
        mx_rest = sb("mx_rest", [P, 2, TT, H // 2])
        mx_part = [sb(f"mx_part{i}", [P, TT, 3, H // 2], BF16) for i in range(2)]
        mx_t = [sb(f"mx_t{i}", [3 * H // 2, S], BF16) for i in range(2)]
        prob = sb("prob", [P, 8, 2 * S])
        o_sb = sb("o_sb", [P, H // 4, S])
        den_r = sb("den_r", [P, TT, H])
        ctx_sb = sb("ctx_sb", [P, TT, D])
        ctx_t = sb("ctx_t", [P, S])
        att_tmp = sb("att_tmp", [P, TT, D])
        gate_a = [sb(f"gate_a{i}", [P, D]) for i in range(2)]
        gate_b = [sb(f"gate_b{i}", [P, D]) for i in range(2)]
        h2_t = 2 * [sb("h2_t", [P, S])]
        h2_hi = [sb(f"h2_hi{i}", [P, S], F32R) for i in range(2)]
        h2_lo = [sb(f"h2_lo{i}", [P, S], F32R) for i in range(2)]
        lg = sb("lg", [P, TT, E + 1])
        top8 = sb("top8", [P, TT, 8])
        idx8 = sb("idx8", [P, TT, 8], U32)
        idx_f = sb("idx_f", [P, TT, 2])
        dz = sb("dz", [P, 2, TT])
        dz_th = sb("dz_th", [P, 2, TT])
        w_top = sb("w_top", [P, 2, TT])
        sh_gate = sb("sh_gate", [P, TT])
        hot1 = sb("hot1", [P, TT, E])
        hot2 = sb("hot2", [P, TT, E])
        score = sb("score", [P, TT, E])
        score_t = sb("score_t", [E, S])
        g_sb = sb("g_sb", [P, CW])
        th_sb = sb("th_sb", [P, CW])
        u_sb = sb("u_sb", [P, CW])
        glu_sb = [sb(f"glu_sb{i}", [P, CW]) for i in range(2)]
        uw_sb = sb("uw_sb", [P, CW])
        act_w = [sb(f"act_w{i}", [P, CW]) for i in range(2)]
        act_ts = sb("act_ts", [P, NQ, CW // P, P])
        act_t = [act_ts[:, q] for q in range(NQ)]
        sh_th = sb("sh_th", [P, FS])
        sh_glu = sb("sh_glu", [P, FS])
        sh_act = sb("sh_act", [P, FS])
        sh_t = [sb(f"sh_t{i}", [P, FS // P, P]) for i in range(TT)]
        ffn_tmp = sb("ffn_tmp", [P, TT, D])

        wgu = [prob[:, 4 * l:4 * l + 4, :].rearrange("p (g a) c -> p g (a c)", g=2) for l in range(2)]
        wsgu = g_sb[:].rearrange("p (g f) -> p g f", g=2)
        spare = act_ts[:].rearrange("p q a b -> p (q a b)")
        wmod = [spare[:, 8 * P * l:8 * P * l + 6 * D] for l in range(2)]
        whole = lambda buf: buf[:].rearrange("p a b -> p (a b)")
        g_up, g_down, g_pos, g_neg = (
            [whole(o_sb)[0:B, i * S:i * S + 2 * D], part[0:B, :]]
            for i, part in enumerate((whole(ctx_sb), whole(att_tmp), spare[:, 6 * P:8 * P], spare[:, 14 * P:16 * P])))

        def dram(name, shape, dt):
            return nc.dram_tensor(name, shape, dt, kind="Internal").ap()

        gate_dram = [dram(f"gate_dram{l}", (B, 2 * D), F32) for l in range(2)]
        bias_dram = dram("bias_dram", (E, 3, 2 * F), BF16)
        ali_dram = dram("ali_dram", (H, 3, S), BF16)
        part_dram = [dram(f"part_dram{i}", (2, P, NJ, S), BF16) for i in range(2)]
        max_dram = [dram(f"max_dram{i}", (3, 2, H // 4, S), BF16) for i in range(2)]

        first_loaded, x_first, rest_loaded, x_rest = sem("first_loaded"), sem("x_first"), sem("rest_loaded"), sem("x_rest")
        pool_const = sem("pool_const")
        pool_mask = sem("pool_mask")
        dve_const = sem("dve_const")
        c_tanh = sem("c_tanh")
        c_silu = sem("c_silu")
        mod_mm, mod_ok = sem("mod_mm"), sem("mod_ok")
        gate_ok, gate_stored = sem("gate_ok"), sem("gate_stored")
        bias_ok, bias_stored, bias_back = sem("bias_ok"), sem("bias_stored"), sem("bias_back")
        ali_ok, ali_stored, ali_back = sem("ali_ok"), sem("ali_stored"), sem("ali_back")
        bov_mm, bov_ok = sem("bov_mm"), sem("bov_ok")
        zeros_in = sem("zeros_in")
        wgu_rounded, wgu_rest = sem("wgu_rounded"), sem("wgu_rest")

        ln_done = [sem("ln1_done"), sem("ln2_done")]
        ln_rstd = [sem("ln1_rstd"), sem("ln2_rstd")]
        h_mm, h_ok = sem("h_mm"), sem("h_ok")
        qk_mm, qk_ok = sem("qk_mm"), sem("qk_ok")
        qk_hi, qk_r, qk_mid, qk_lo = sem("qk_hi"), sem("qk_r"), sem("qk_mid"), sem("qk_lo")
        parts_stored = sem("parts_stored")
        stk_loaded = [sem("stk_loaded0"), sem("stk_loaded1")]
        v_mm, v_ok = sem("v_mm"), sem("v_ok")
        s_mm, max_done = sem("s_mm"), sem("max_done")
        mx_split = sem("mx_split")
        mxt_mm, mxt_ok = sem("mxt_mm"), sem("mxt_ok")
        mx_stored = [sem("mx_stored0"), sem("mx_stored1")]
        mx_loaded = [sem("mx_loaded0"), sem("mx_loaded1")]
        st_mm, exp_done = sem("st_mm"), sem("exp_done")
        av_mm, o_ok = sem("av_mm"), sem("o_ok")
        ot_mm, ctx_norm = sem("ot_mm"), sem("ctx_norm")
        ctx_mm, ctx_ok = sem("ctx_mm"), sem("ctx_ok")
        wo_mm, att_scaled, att_added = sem("wo_mm"), sem("att_scaled"), sem("att_added")
        gate_a_in, gate_b_in = ([sem(f"{n}{i}") for i in range(2)] for n in ("gate_a_in", "gate_b_in"))
        h2_mm, h2_ok, rt_mm = sem("h2_mm"), sem("h2_ok"), sem("rt_mm")
        h2_rounded, h2_rest = sem("h2_rounded"), sem("h2_rest")
        top_step = sem("top_step")
        z_ok, sg_ok = sem("z_ok"), sem("sg_ok")
        top_tanh = sem("top_tanh")
        score_step = sem("score_step")
        sct_mm, sct_ok = sem("sct_mm"), sem("sct_ok")
        g_mm, u_mm, th_ok = sem("g_mm"), sem("u_mm"), sem("th_ok")
        g_clip = sem("g_clip")
        u_taken, uw_ok = sem("u_taken"), sem("uw_ok")
        glu_ok, actw_ok = sem("glu_ok"), sem("actw_ok")
        at_mm, at_ok = sem("at_mm"), sem("at_ok")
        sh_mm, sh_th_ok, sh_glu_ok, sh_act_ok = sem("sh_mm"), sem("sh_th_ok"), sem("sh_glu_ok"), sem("sh_act_ok")
        sht_mm, sht_ok = sem("sht_mm"), sem("sht_ok")
        dn_mm, ffn_scaled, ffn_added = sem("dn_mm"), sem("ffn_scaled"), sem("ffn_added")
        out_stored = sem("out_stored")

        TAKEN = {
            "act_t0": (at_ok, 4, 1), "act_t1": (at_ok, 4, 2), "act_t2": (at_ok, 4, 3), "act_t3": (at_ok, 4, 4),
            "max_t0": (mxt_ok, 2, 1), "max_t1": (mxt_ok, 2, 2), "h_t": (h_ok, 1, 1), "qk": (qk_ok, 2, 2),
            "o_t0": (ctx_norm, 4, 2), "o_t1": (ctx_norm, 4, 4), "down0": (ffn_scaled, 2, 1), "down1": (ffn_scaled, 2, 2),
            "v": (v_ok, 1, 1), "ctx_t": (ctx_ok, 1, 1), "score_t": (sct_ok, 1, 1), "wo": (att_scaled, 1, 1),
            "h2_t": (h2_ok, 1, 1), "router": (top_step, 9, 1), "sh_t0": (sht_ok, 2, 1), "sh_t1": (sht_ok, 2, 2),
        }

        FIRST_LOADS = 7
        REST_LOADS = 21
        GATE_STEPS = 5
        SPLIT_B = 8

        block = ctx.enter_context(nc.Block())

        @block.sync
        def _(sp):
            sp.dma_start(c_t[0][:], io["c0"]).then_inc(first_loaded, 16)
            sp.dma_start(wmod[0], io["wmod0"]).then_inc(first_loaded, 16)
            x_dram = io["x"].rearrange("b (t p) d -> p b t d", p=P)
            for t in range(TT):
                sp.dma_start(x[:, 0:SPLIT_B, t, :], x_dram[:, 0:SPLIT_B, t, :]).then_inc(x_first, 16)
            for dst, name in ((wq[0], "wq0"), (wk[0], "wk0"), (bq, "bq"), (bk, "bk"), (slopes, "slopes")):
                sp.dma_start(dst[:], io[name]).then_inc(first_loaded, 16)
            for dst, name in ((b_in, "b_gu"), (wv[0], "wv0"), (wo[0], "wo0"), (bv, "bv"), (bo, "bo"), (bd, "bd"),
                              (wr[0], "wr0"), (wgu[0], "wgu0"),
                              (wd[0], "wd0"), (c_t[1], "c1"), (wmod[1], "wmod1"), (wq[1], "wq1"), (wk[1], "wk1"),
                              (wv[1], "wv1"), (wo[1], "wo1"), (wgu[1], "wgu1"), (wd[1], "wd1"), (wsgu, "wsgu"),
                              (wsd, "wsd")):
                sp.dma_start(dst[:] if name[:4] not in ("wgu0", "wgu1", "wmod", "wsgu") else dst, io[name]).then_inc(rest_loaded, 16)
            sp.dma_start(wr[1][:, 0:E], io["wr1"]).then_inc(rest_loaded, 16)
            sp.dma_start(wr[1][:, E:E + 1], io["wsg"]).then_inc(rest_loaded, 16)
            sp.wait_ge(ali_ok, 6)
            sp.dma_start(ali_dram, ali_part[:]).then_inc(ali_stored, 16)
            sp.wait_ge(gate_ok, GATE_STEPS)
            sp.dma_start(gate_dram[0], g_row[0][:]).then_inc(gate_stored, 16)
            sp.wait_ge(ali_stored, 16)
            sp.wait_ge(dve_const, 2)
            ali_rows = ali_dram.rearrange("(h par) j t -> par j h t", par=2)
            for i in range(2):
                for par in range(2):
                    r0 = 64 * par + R_PROD
                    sp.dma_start(k_stk[0][i][r0:r0 + 3], ali_rows[par]).then_inc(ali_back, 16)

            def second_setup():
                sp.wait_ge(gate_stored, 16)
                sp.wait_ge(gate_ok, 2 * GATE_STEPS)
                sp.dma_start(gate_dram[1], g_row[1][:]).then_inc(gate_stored, 16)
                sp.wait_ge(bias_ok, 6)
                sp.dma_start(bias_dram, b_part[:]).then_inc(bias_stored, 16)
                for t in range(TT):
                    sp.dma_start(x[:, SPLIT_B:B, t, :], x_dram[:, SPLIT_B:B, t, :]).then_inc(x_rest, 16)
                sp.wait_ge(bias_stored, 16)
                sp.wait_ge(dve_const, 5)
                for k in k_stk[1]:
                    for par in range(2):
                        r0 = 64 * par + R_PROD
                        sp.dma_start(k[r0:r0 + 3].rearrange("r h t -> r (h t)"), b_stack[64:67, :]).then_inc(zeros_in, 16)
                for gu in range(2):
                    sp.dma_start(b_stack[0:3, gu * E * F:(gu + 1) * E * F].rearrange("j (e f) -> j e f", f=F),
                                 bias_dram[:, :, gu * F:(gu + 1) * F].rearrange("e j f -> j e f")).then_inc(bias_back, 16)
                sp.wait_ge(gate_stored, 32)

            def max_rows(u, half):
                ready = apart(sp, pool_const, u.count(2, 1 + half))
                sp.wait_ge(mxt_ok, ready)
                if u.has(1):
                    ready = apart(sp, pool_const, u.count(32, 0))
                    sp.wait_ge(mx_loaded[half], ready)
                sp.dma_start(max_dram[half].rearrange("j par h t -> (j par h) t"), mx_t[half][:])\
                  .then_inc(mx_stored[half], 16)
                ready = apart(sp, pool_const, u.count(16, 16))
                sp.wait_ge(mx_stored[half], ready)
                for par in range(2):
                    r0 = 64 * par + R_BIAS
                    sp.dma_start(q_stk[u.par][r0:r0 + 3, half * 4:half * 4 + 4, :], max_dram[half][:, par])\
                      .then_inc(mx_loaded[half], 16)

            def stack_rows(u, half):
                for qk in range(2):
                    dst = (q_stk[u.par], k_stk[u.layer][u.par])[qk]
                    src = part_dram[u.par][qk].rearrange("(h par d) j t -> par (d j) h t", par=2, d=DH)
                    for par in range(2):
                        sp.dma_start(dst[64 * par:64 * par + R_PROD, half * 4:half * 4 + 4, :],
                                     src[par, :, half * 4:half * 4 + 4, :]).then_inc(stk_loaded[half], 16)

            for u0, u1, u2, u3, u4, u5 in iterations(sp):
                if u0.first == 1:
                    second_setup()
                if u2.live:
                    if u2.has(2):
                        ready = apart(sp, pool_const, u2.count(1, -1))
                        sp.wait_ge(att_scaled, ready)
                    sp.dma_start(gate_a[u2.par][:], gate_dram[u2.layer][bass.ds(u2.batch, 1), 0:D].broadcast_to([P, D]))\
                      .then_inc(gate_a_in[u2.par], 16)
                    max_rows(u2, 1)
                if u3.live:
                    if u3.has(2):
                        ready = apart(sp, pool_const, u3.count(2, -2))
                        sp.wait_ge(ffn_scaled, ready)
                    sp.dma_start(gate_b[u3.par][:], gate_dram[u3.layer][bass.ds(u3.batch, 1), D:2 * D].broadcast_to([P, D]))\
                      .then_inc(gate_b_in[u3.par], 16)
                if u5.live and u5.layer == 1:
                    ready = apart(sp, pool_const, u5.count(2, 2))
                    sp.wait_ge(ffn_added, ready)
                    sp.dma_start(out[bass.ds(u5.batch, 1)].rearrange("b (t p) d -> p (b t) d", p=P),
                                 x[:, bass.ds(u5.batch, 1), :, :].rearrange("p b t d -> p (b t) d")).then_inc(out_stored, 16)
                if u0.live:
                    ready = apart(sp, pool_const, u0.count(1, 1))
                    sp.wait_ge(qk_lo, ready)
                    if u0.has(2):
                        for half in range(2):
                            ready = apart(sp, pool_const, u0.count(64, -64))
                            sp.wait_ge(stk_loaded[half], ready)
                    dst = part_dram[u0.par]
                    for j0, nj, part in ((0, 3, 0), (3, 2, 1), (5, 1, 2)):
                        sp.dma_start(dst[0, :, j0:j0 + nj, :],
                                     qk_part[:, part:part + 1, 0:S].broadcast_to([P, nj, S])).then_inc(parts_stored, 16)
                    for j0, nj in ((0, 3), (3, 2), (5, 1)):
                        sp.dma_start(dst[1, :, j0:j0 + nj, :], qk_part[:, 0:nj, S:2 * S]).then_inc(parts_stored, 16)
                    ready = apart(sp, pool_const, u0.count(96, 96))
                    sp.wait_ge(parts_stored, ready)
                    if u0.first == 0:
                        sp.wait_ge(dve_const, 3)
                    if u0.has(2):
                        ready = apart(sp, pool_const, u0.count(16, -32 + 8))
                        sp.wait_ge(st_mm, ready)
                    stack_rows(u0, 0)
                if u1.live:
                    max_rows(u1, 0)
                if u0.live:
                    if u0.has(2):
                        ready = apart(sp, pool_const, u0.count(16, -16))
                        sp.wait_ge(st_mm, ready)
                    stack_rows(u0, 1)
            sp.wait_ge(out_stored, 16 * B)

        @block.gpsimd
        def _(pool):
            pool.wait_ge(dve_const, 1)
            pool.affine_select(out=ident[:], in_=ident[:], compare_op=ALU.not_equal, fill=1.0, base=0,
                               pattern=[[-1, P]], channel_multiplier=1).then_inc(pool_mask, 1)
            pool.wait_ge(pool_mask, 1)
            pool.iota(pos[:], [[1, S]], base=-(S - 1), channel_multiplier=0, allow_small_or_imprecise_dtypes=True)\
                .then_inc(pool_const, 1)
            pool.iota(iota_e[:], [[1, E]], base=0, channel_multiplier=0, allow_small_or_imprecise_dtypes=True)\
                .then_inc(pool_const, 1)

            def rstd(u, i):
                ready = apart(pool, dve_const, u.count(6, 4))
                pool.wait_ge(ln_done[i], ready)
                pool.tensor_scalar(ln_ve[i][:], ln_mv[i][:, :, 1], EPS, None, ALU.add).then_inc(ln_rstd[i], 1)
                pool.wait_ge(ln_rstd[i], u.count(2, 1))
                pool.tensor_tensor(ln_rs[i][:], ln_ve[i][:], neg_half[:], ALU.pow).then_inc(ln_rstd[i], 1)

            def weigh(u, q):
                t, e0 = q // 2, (q % 2) * EC
                pool.wait_ge(u_taken, u.count(4, q + 1))
                if q == 0:
                    pool.wait_ge(score_step, u.count(5, 5))
                if u.has(1) or q:
                    pool.wait_ge(actw_ok, u.count(4, q))
                pool.tensor_tensor(uw_sb[:].rearrange("p (e f) -> p e f", f=F),
                                   u_sb[:].rearrange("p (e f) -> p e f", f=F),
                                   score[:, t, e0:e0 + EC].rearrange("p (e o) -> p e o", o=1).broadcast_to([P, EC, F]),
                                   ALU.mult).then_inc(uw_ok, 1)
                pool.wait_ge(glu_ok, u.count(4, q + 1))
                pool.wait_ge(uw_ok, u.count(4, q + 1))
                if u.has(1) or q >= 2:
                    pool.wait_ge(at_mm, u.count(4, q - 1))
                pool.tensor_tensor(act_w[q % 2][:], uw_sb[:], glu_sb[q % 2][:], ALU.mult).then_inc(actw_ok, 1)

            def second_setup():
                for l in range(2):
                    pool.wait_ge(wgu_rounded, l + 1)
                    pool.tensor_tensor(wgu_lo[l][:], wgu[l], wgu_hi[l][:], ALU.subtract).then_inc(wgu_rest, 1)
                pool.wait_ge(wgu_rounded, 3)
                pool.tensor_tensor(wsgu_lo[:], wsgu, wsgu_hi[:], ALU.subtract).then_inc(wgu_rest, 1)

            for u0, u1, u2, u3, u4, u5 in iterations(pool):
                if u0.first == 1:
                    second_setup()
                if u0.live:
                    rstd(u0, 0)
                if u4.live:
                    ready = apart(pool, dve_const, u4.count(9, 9))
                    pool.wait_ge(top_step, ready)
                    if u4.layer == 0 and u4.has(1):
                        pool.wait_ge(sct_mm, u4.count(1, 0))
                    for t in range(TT):
                        for k, hot in ((0, hot1), (1, hot2)):
                            pool.tensor_scalar(hot[:, t, :], iota_e[:], idx_f[:, t, k:k + 1], w_top[:, k, t:t + 1],
                                               ALU.is_equal, ALU.mult).then_inc(score_step, 1)
                    pool.wait_ge(score_step, u4.count(5, 4))
                    pool.tensor_tensor(score[:], hot1[:], hot2[:], ALU.add).then_inc(score_step, 1)
                    weigh(u4, 0)
                if u0.live:
                    pool.wait_ge(qk_hi, u0.count(1, 1))
                    pool.tensor_tensor(qk_rest[:], qk_f[:], qk_part[:, 0, :], ALU.subtract).then_inc(qk_r, 1)
                    pool.wait_ge(qk_mid, u0.count(1, 1))
                    pool.tensor_tensor(qk_part[:, 2, :], qk_rest[:], qk_part[:, 1, :], ALU.subtract).then_inc(qk_lo, 1)
                if u4.live:
                    weigh(u4, 1)
                if u5.live:
                    ready = apart(pool, dve_const, u5.count(2, 2))
                    pool.wait_ge(ffn_scaled, ready)
                    xt = x[:, bass.ds(u5.batch, 1), 1, :]
                    pool.tensor_tensor(xt, xt, ffn_tmp[:, 1:2, :], ALU.add).then_inc(ffn_added, 1)
                if u3.live:
                    ready = apart(pool, dve_const, u3.count(1, 1))
                    pool.wait_ge(att_scaled, ready)
                    xt = x[:, bass.ds(u3.batch, 1), :, :].rearrange("p b t d -> p (b t) d")
                    pool.tensor_tensor(xt, xt, att_tmp[:], ALU.add).then_inc(att_added, 1)
                    rstd(u3, 1)
                if u4.live:
                    weigh(u4, 2)
                    ready = apart(pool, dve_const, u4.count(2, 1))
                    pool.wait_ge(ffn_scaled, ready)
                    xt = x[:, bass.ds(u4.batch, 1), 0, :]
                    pool.tensor_tensor(xt, xt, ffn_tmp[:, 0:1, :], ALU.add).then_inc(ffn_added, 1)
                    weigh(u4, 3)

        @block.scalar
        def _(act):
            act.wait_ge(first_loaded, 16 * FIRST_LOADS)
            act.activation(c_th[0][:], c_t[0][:], ACT.Tanh, scale=0.5).then_inc(c_tanh, 1)
            act.activation(bq_s[:], bq[:], ACT.Copy, scale=SCALE).then_inc(c_tanh, 1)
            act.wait_ge(c_tanh, 2)
            act.wait_ge(mod_ok, 2)

            def second_setup():
                act.wait_ge(rest_loaded, 16 * REST_LOADS)
                act.activation(c_th[1][:], c_t[1][:], ACT.Tanh, scale=0.5).then_inc(c_tanh, 1)
                for l in range(2):
                    act.activation(wgu_hi[l][:], wgu[l], ACT.Copy).then_inc(wgu_rounded, 1)
                act.activation(wsgu_hi[:], wsgu, ACT.Copy).then_inc(wgu_rounded, 1)

            def tanh_top(u):
                act.wait_ge(top_step, u.count(9, 7))
                if u.layer == 1:
                    act.wait_ge(z_ok, u.count1(1, 1))
                n = 1 + u.layer
                act.activation(dz_th[:, 0:n, :], dz[:, 0:n, :], ACT.Tanh, scale=0.5).then_inc(top_tanh, 1)

            def tanh_gate(u, q):
                if u.layer == 0:
                    act.wait_ge(g_clip, u.count(4, q + 1))
                else:
                    act.wait_ge(g_mm, u.count(4, q + 1))
                if u.has(1) or q:
                    act.wait_ge(glu_ok, u.count(4, q))
                if u.layer == 0:
                    act.activation(th_sb[:], g_sb[:], ACT.Tanh, scale=0.5 * ALPHA).then_inc(th_ok, 1)
                else:
                    act.activation(th_sb[:], ps_g[:], ACT.Tanh, scale=0.5).then_inc(th_ok, 1)

            def take_up(u, q):
                if u.layer == 1:
                    act.wait_ge(u_mm, u.count(4, q + 1))
                    act.wait_ge(uw_ok, u.count(4, q))
                    act.activation(u_sb[:], ps_u[:], ACT.Copy).then_inc(u_taken, 1)

            def tanh_shared(u, t):
                if u.layer == 1:
                    act.wait_ge(sh_mm, u.count1(2, t + 1))
                    act.activation(sh_th[:], ps_g[:, 0:FS], ACT.Tanh, scale=0.5).then_inc(sh_th_ok, 1)

            def take_act_t(u, q):
                act.wait_ge(at_mm, u.count(4, q + 1))
                act.activation(act_t[q].rearrange("p a b -> p (a b)"), ps_job[BANK[f"act_t{q}"]][:], ACT.Copy)\
                   .then_inc(at_ok, 1)

            def take_sh_t(u, t):
                if u.layer == 1:
                    act.wait_ge(sht_mm, u.count1(2, t + 1))
                    act.activation(sh_t[t][:].rearrange("p a b -> p (a b)"), ps_job[BANK[f"sh_t{t}"]][:, 0:FS], ACT.Copy)\
                       .then_inc(sht_ok, 1)

            def take_max_t(u, half):
                act.wait_ge(mxt_mm, u.count(2, half + 1))
                if u.has(1):
                    act.wait_ge(mx_stored[half], u.count(16, 0))
                act.activation(mx_t[half][:], ps_job[BANK[f"max_t{half}"]][:].bitcast(BF16)[0:3 * H // 2, 0:S], ACT.Copy)\
                   .then_inc(mxt_ok, 1)

            def take_h(u, i, mm, ok, dst, job):
                act.wait_ge(mm, u.count(1, 1))
                act.activation(dst[u.par][:], ps_job[BANK[job]][:, 0:S], ACT.Identity,
                               scale=mod[u.layer][:, 2 * i + 1, bass.ds(u.batch, 1)],
                               bias=mod[u.layer][:, 2 * i, bass.ds(u.batch, 1)]).then_inc(ok, 1)
                if i == 1:
                    act.wait_ge(ok, u.count(1, 1))
                    act.activation(h2_hi[u.par][:], dst[u.par][:], ACT.Copy).then_inc(h2_rounded, 1)

            def take_o(u, phase):
                act.wait_ge(av_mm, u.count(4, 2 * phase + 2))
                if phase == 0 and u.has(1):
                    act.wait_ge(ot_mm, u.count(2, 0))
                act.activation(o_sb[:, 2 * phase:2 * phase + 2, :].rearrange("p g s -> p (g s)"), ps_o[:], ACT.Copy)\
                   .then_inc(o_ok, 1)

            def take_qk(u):
                act.wait_ge(qk_mm, u.count(1, 1))
                if u.has(1):
                    act.wait_ge(qk_r, u.count(1, 0))
                b = ps_job[BANK["qk"]]
                if u.layer == 0:
                    act.activation(qk_f[:, 0:S], b[:, 0:S], ACT.Identity, scale=SCALE, bias=bq_s[:]).then_inc(qk_ok, 1)
                    act.activation(qk_f[:, S:2 * S], b[:, S:2 * S], ACT.Identity, bias=bk[:]).then_inc(qk_ok, 1)
                else:
                    act.activation(qk_f[:, 0:S], b[:, 0:S], ACT.Copy, scale=SCALE).then_inc(qk_ok, 1)
                    act.activation(qk_f[:, S:2 * S], b[:, S:2 * S], ACT.Copy).then_inc(qk_ok, 1)

            for u0, u1, u2, u3, u4, u5 in iterations(act):
                if u0.first == 1:
                    second_setup()
                if u0.live and u0.first == B:
                    act.wait_ge(mod_ok, 4)
                for k in range(H):
                    if u2.live:
                        act.wait_ge(st_mm, u2.count(16, k + 1))
                        if k >= 8:
                            act.wait_ge(av_mm, u2.count(4, (k - 8) // 4 + 1))
                        elif u2.has(1):
                            act.wait_ge(av_mm, u2.count(4, (k + 8) // 4 - 3))
                        act.activation(prob[:, k % 8, :], ps_st[k % 2][:], ACT.Exp).then_inc(exp_done, 1)
                    if k == 3:
                        if u0.live:
                            take_h(u0, 0, h_mm, h_ok, h_t, "h_t")
                        if u2.live:
                            take_max_t(u2, 1)
                    if k == 11 and u4.live:
                        take_act_t(u4, 1)
                        take_sh_t(u4, 0)
                    if u4.live:
                        for q in range(NQ):
                            if k == GATE_STEP[u4.layer][q] + 1 - u4.layer:
                                tanh_gate(u4, q)
                            if k == UP_STEP[q] + 1:
                                take_up(u4, q)
                        for t in range(TT):
                            if k == SHARED_STEP[t]:
                                tanh_shared(u4, t)
                    if k == 1 and u5.live:
                        take_act_t(u5, 3)
                    if k == 2:
                        if u5.live:
                            take_sh_t(u5, 1)
                        if u3.live:
                            take_o(u3, 1)
                    if k == 3 and u4.live:
                        tanh_top(u4)
                    if k == 4 and u0.live:
                        take_qk(u0)
                    if k == 5 and u0.live:
                        act.wait_ge(qk_ok, u0.count(2, 2))
                        if u0.has(1):
                            act.wait_ge(parts_stored, u0.count(96, 0))
                        act.activation(qk_part[:, 0, :], qk_f[:], ACT.Copy).then_inc(qk_hi, 1)
                    if k == 6:
                        if u1.live:
                            act.wait_ge(v_mm, u1.count(1, 1))
                            act.activation(v_ext[u1.par][:, :, :, 0:DH],
                                           ps_job[BANK["v"]][:, 0:S].rearrange("p (t h d) -> p t h d", t=TT, h=H),
                                           ACT.Copy).then_inc(v_ok, 1)
                    if k == 7:
                        if u0.live:
                            act.wait_ge(qk_r, u0.count(1, 1))
                            act.activation(qk_part[:, 1, :], qk_rest[:], ACT.Copy).then_inc(qk_mid, 1)
                        if u3.live:
                            act.wait_ge(ctx_mm, u3.count(1, 1))
                            act.activation(ctx_t[:], ps_job[BANK["ctx_t"]][:, 0:S], ACT.Copy).then_inc(ctx_ok, 1)
                    if k == 8 and u4.live:
                        take_act_t(u4, 0)
                    if k == 9 and u4.live and u4.layer == 0:
                        act.wait_ge(sct_mm, u4.count(1, 1))
                        act.activation(score_t[:], ps_job[BANK["score_t"]][0:E, 0:S], ACT.Copy).then_inc(sct_ok, 1)
                    if k == 10:
                        if u2.live:
                            take_o(u2, 0)
                        if u1.live:
                            take_max_t(u1, 0)
                    if k == 14:
                        if u4.live:
                            take_act_t(u4, 2)
                        if u3.live:
                            take_h(u3, 1, h2_mm, h2_ok, h2_t, "h2_t")
        @block.tensor
        def _(pe):
            def modulation(l):
                pe.wait_ge(c_silu, 2 * l + 2)
                for i, ch in enumerate((0, 1, 3, 4)):
                    pe.matmul(ps_g[:, i * B:(i + 1) * B], wmod[l][:, ch * D:(ch + 1) * D], c_si[l][:],
                              start=True, stop=True)
                for i, ch in enumerate((2, 5)):
                    mm = pe.matmul(ps_u[0:B, i * D:(i + 1) * D], c_si[l][:], wmod[l][:, ch * D:(ch + 1) * D],
                                   start=True, stop=True)
                mm.then_inc(mod_mm, 1)

            def second_setup():
                pe.wait_ge(rest_loaded, 16 * REST_LOADS)
                pe.wait_ge(mod_ok, 2)
                pe.wait_ge(gate_ok, GATE_STEPS)
                modulation(1)
                pe.matmul(ps_o[0:1, 0:D], bv[:], wo[0][:], start=True, stop=True).then_inc(bov_mm, 1)
                pe.wait_ge(bov_ok, 1)
                pe.wait_ge(mod_ok, 4)
                pe.wait_ge(gate_ok, 2 * GATE_STEPS)
                pe.wait_ge(ali_back, 64)
                pe.wait_ge(dve_const, 5)

            pe.wait_ge(first_loaded, 16 * FIRST_LOADS)
            modulation(0)
            pe.wait_ge(dve_const, 4)
            pe.wait_ge(pool_const, 1)

            now = []

            def job(name):
                names = [n for n, _, _, _ in JOBS]
                at = names.index(name)
                for back in range(1, len(JOBS) + 1):
                    before, lag, layers, b = JOBS[at - back]
                    lag += back > at
                    if b == BANK[name] and lag < LAGS and now[lag].live and now[lag].layer in layers:
                        done, per, c = TAKEN[before]
                        pe.wait_ge(done, now[lag].count1(per, c) if done is sht_ok else now[lag].count(per, c))
                        break
                return ps_job[BANK[name]]

            def chunk_gate(u, q):
                if q == 0:
                    pe.wait_ge(h2_rest, u.count(1, 1))
                if u.layer == 0:
                    if u.has(1) or q:
                        pe.wait_ge(g_clip, u.count(4, q))
                elif q in (0, 2):
                    if u.first == B:
                        pe.wait_ge(g_clip, 4 * B) if q == 0 else pe.wait_ge(sh_act_ok, u.count1(2, 1))
                    else:
                        pe.wait_ge(sh_act_ok, u.count1(2, q // 2))
                else:
                    pe.wait_ge(glu_ok, u.count(4, q))
                chunk(u, q, ps_g, 0).then_inc(g_mm, 1)

            def chunk_up(u, q):
                if u.has(1) or q:
                    pe.wait_ge(u_taken, u.count(4, q))
                chunk(u, q, ps_u, 1).then_inc(u_mm, 1)

            def chunk(u, q, dst, gu):
                t, c0 = q // 2, (q % 2) * CW
                if u.layer == 0:
                    pe.matmul(dst[:], ones_b[:], b_stack[:, gu * E * F + c0:gu * E * F + c0 + CW], start=True, stop=False)
                parts = ((h2_hi, wgu_hi), (h2_hi, wgu_lo), (h2_lo, wgu_hi))
                for i, (h, w) in enumerate(parts):
                    mm = pe.matmul(dst[:], h[u.par][:, t * P:(t + 1) * P], w[u.layer][:, gu, c0:c0 + CW],
                                   start=u.layer == 1 and i == 0, stop=i == len(parts) - 1)
                return mm

            def shared(u, t):
                if u.layer == 1:
                    pe.wait_ge(glu_ok, u.count(4, 2 * t + 2))
                    parts = ((h2_hi, wsgu_hi), (h2_hi, wsgu_lo), (h2_lo, wsgu_hi))
                    for i, (h, w) in enumerate(parts):
                        mm = pe.matmul(ps_g[:], h[u.par][:, t * P:(t + 1) * P], w[:].rearrange("p g f -> p (g f)"),
                                       start=i == 0, stop=i == len(parts) - 1)
                    mm.then_inc(sh_mm, 1)

            def act_transpose(u, q):
                pe.wait_ge(actw_ok, u.count(4, q + 1))
                b = job(f"act_t{q}")
                for j in range(CW // P):
                    mm = pe.transpose(b[:, j * P:(j + 1) * P], act_w[q % 2][:, j * P:(j + 1) * P], ident[:])
                mm.then_inc(at_mm, 1)

            def sh_transpose(u, t):
                if u.layer == 1:
                    pe.wait_ge(sh_act_ok, u.count1(2, t + 1))
                    b = job(f"sh_t{t}")
                    for j in range(FS // P):
                        mm = pe.transpose(b[:, j * P:(j + 1) * P], sh_act[:, j * P:(j + 1) * P], ident[:])
                    mm.then_inc(sht_mm, 1)

            def down(u, t):
                pe.wait_ge(at_ok, u.count(4, 2 * t + 2))
                if u.layer == 0:
                    if t == 0:
                        pe.wait_ge(sct_ok, u.count(1, 1))
                else:
                    pe.wait_ge(sht_ok, u.count1(2, t + 1))
                b = job(f"down{t}")
                pairs = [(act_t[2 * t + j // 4][:, j % 4, :], wd[u.layer][:, j, :]) for j in range(E // 2)]
                if u.layer == 0:
                    pairs.append((score_t[:, t * P:(t + 1) * P], bd2[:]))
                else:
                    pairs += [(sh_t[t][:, j, :], wsd[:, j, :]) for j in range(FS // P)]
                for j, (lhs_t, rhs) in enumerate(pairs):
                    mm = pe.matmul(b[:, 0:D], lhs_t, rhs, start=j == 0, stop=j == len(pairs) - 1)
                mm.then_inc(dn_mm, 1)

            def max_transpose(u, half):
                pe.wait_ge(mx_split, u.count(8, 4 * half + 4))
                b = job(f"max_t{half}")
                for t in range(TT):
                    mm = pe.transpose(b[:].bitcast(BF16)[0:3 * H // 2, t * P:(t + 1) * P],
                                      mx_part[half][:, t].rearrange("p j h -> p (j h)"), ident_b[:])
                mm.then_inc(mxt_mm, 1)

            def probs_values(u, g):
                pe.wait_ge(exp_done, u.count(16, 4 * g + 4))
                if g == 0:
                    pe.wait_ge(v_ok, u.count(1, 1))
                if g % 2 == 0 and (u.has(1) or g):
                    pe.wait_ge(o_ok, u.count(2, g // 2))
                for kt in range(TT):
                    for i in range(4):
                        h = 4 * g + i
                        mm = pe.matmul(ps_o[32 * i:32 * i + 32, (g % 2) * S:(g % 2 + 1) * S], v_ext[u.par][:, kt, h, :],
                                       prob[:, h % 8, kt * S:(kt + 1) * S], start=g % 2 == 0 and kt == 0,
                                       stop=kt == TT - 1, skip_group_check=True)
                mm.then_inc(av_mm, 1)

            def out_transpose(u, t):
                if t == 0:
                    pe.wait_ge(o_ok, u.count(2, 2))
                b = job(f"o_t{t}")
                for g in range(H // 4):
                    mm = pe.transpose(b[:, g * P:(g + 1) * P], o_sb[:, g, t * P:(t + 1) * P], ident[:])
                mm.then_inc(ot_mm, 1)

            def norm_transpose(u, i, name, done):
                pe.wait_ge(ln_done[i], u.count(6, 6))
                b = job(name)
                for t in range(TT):
                    mm = pe.transpose(b[:, t * P:(t + 1) * P], xn[i][:, t, :], ident[:])
                mm.then_inc(done, 1)

            for u0, u1, u2, u3, u4, u5 in iterations(pe):
                if u0.first == 1:
                    second_setup()
                if u0.first == B:
                    pe.wait_ge(zeros_in, 16 * 4)
                now[:] = [u0, u1, u2, u3, u4, u5]
                for k in range(H):
                    hp, par = k // 2, k % 2
                    r0 = 64 * par
                    if u1.live:
                        if k % 8 == 0:
                            pe.wait_ge(stk_loaded[k // 8], u1.count(64, 64))
                        if k or u1.has(1):
                            pe.wait_ge(max_done, u1.count(16, k))
                        q, kk = q_stk[u1.par], k_stk[u1.layer][u1.par]
                        for t in range(TT):
                            mm = pe.matmul(ps_s[:, t * S:(t + 1) * S], q[r0:r0 + R_BIAS, hp, t * P:(t + 1) * P],
                                           kk[r0:r0 + R_BIAS, hp, :], start=True, stop=True)
                        mm.then_inc(s_mm, 1)
                    if u2.live:
                        if k % 8 == 0:
                            pe.wait_ge(mx_loaded[k // 8], u2.count(32, 32))
                        if k >= 2 or u2.has(1):
                            pe.wait_ge(exp_done, u2.count(16, k - 1))
                        q, kk = q_stk[u2.par], k_stk[u2.layer][u2.par]
                        for t in range(TT):
                            mm = pe.matmul(ps_st[k % 2][:, t * S:(t + 1) * S], kk[r0:r0 + R_MAX, hp, t * P:(t + 1) * P],
                                           q[r0:r0 + R_MAX, hp, :], start=True, stop=True)
                        mm.then_inc(st_mm, 1)
                    if k == 3:
                        if u0.live:
                            norm_transpose(u0, 0, "h_t", h_mm)
                        if u2.live:
                            max_transpose(u2, 1)
                    if k == 11 and u4.live:
                        act_transpose(u4, 1)
                        sh_transpose(u4, 0)
                    if u4.live:
                        if u4.first == 0 and k == 0:
                            pe.wait_ge(bias_back, 32)
                            pe.wait_ge(wgu_rest, 3)
                        for q in range(NQ):
                            if k == GATE_STEP[u4.layer][q]:
                                chunk_gate(u4, q)
                            if k == UP_STEP[q]:
                                chunk_up(u4, q)
                        for t in range(TT):
                            if k == SHARED_STEP[t]:
                                shared(u4, t)
                    if k == 1:
                        if u3.live:
                            probs_values(u3, 3)
                        if u5.live:
                            act_transpose(u5, 3)
                    if k == 2 and u5.live:
                        sh_transpose(u5, 1)
                    if k == 4:
                        if u0.live:
                            pe.wait_ge(h_ok, u0.count(1, 1))
                            b = job("qk")
                            pe.matmul(b[:, 0:S], wq[u0.layer][:], h_t[u0.par][:], start=True, stop=True)
                            pe.matmul(b[:, S:2 * S], wk[u0.layer][:], h_t[u0.par][:], start=True, stop=True)\
                              .then_inc(qk_mm, 1)
                        if u2.live:
                            probs_values(u2, 0)
                        if u3.live:
                            out_transpose(u3, 0)
                    if k == 6:
                        if u3.live:
                            out_transpose(u3, 1)
                        if u1.live:
                            b = job("v")
                            for t in range(TT):
                                mm = pe.matmul(b[:, t * D:(t + 1) * D], h_t[u1.par][:, t * P:(t + 1) * P],
                                               wv[u1.layer][:], start=True, stop=True)
                            mm.then_inc(v_mm, 1)
                    if k == 7:
                        if u5.live:
                            down(u5, 1)
                        if u3.live:
                            pe.wait_ge(ctx_norm, u3.count(4, 4))
                            b = job("ctx_t")
                            for t in range(TT):
                                mm = pe.transpose(b[:, t * P:(t + 1) * P], ctx_sb[:, t, :], ident[:])
                            mm.then_inc(ctx_mm, 1)
                    if k == 8:
                        if u4.live:
                            act_transpose(u4, 0)
                        if u3.live:
                            pe.wait_ge(ctx_ok, u3.count(1, 1))
                            b = job("wo")
                            for t in range(TT):
                                if u3.layer == 0:
                                    pe.matmul(b[:, t * D:(t + 1) * D], ones_row[:], bo_v[:], start=True, stop=False)
                                mm = pe.matmul(b[:, t * D:(t + 1) * D], ctx_t[:, t * P:(t + 1) * P], wo[u3.layer][:],
                                               start=u3.layer == 1, stop=True)
                            mm.then_inc(wo_mm, 1)
                    if k == 9:
                        if u2.live:
                            probs_values(u2, 1)
                        if u4.live and u4.layer == 0:
                            pe.wait_ge(score_step, u4.count(5, 5))
                            b = job("score_t")
                            for t in range(TT):
                                mm = pe.transpose(b[0:E, t * P:(t + 1) * P], score[:, t, :], ident[:])
                            mm.then_inc(sct_mm, 1)
                    if k == 10 and u1.live:
                        max_transpose(u1, 0)
                    if k == 12 and u4.live:
                        down(u4, 0)
                    if k == 14:
                        if u4.live:
                            act_transpose(u4, 2)
                        if u3.live:
                            norm_transpose(u3, 1, "h2_t", h2_mm)
                    if k == 15:
                        if u2.live:
                            probs_values(u2, 2)
                        if u3.live:
                            pe.wait_ge(h2_ok, u3.count(1, 1))
                            b = job("router")
                            n = E + u3.layer
                            for t in range(TT):
                                mm = pe.matmul(b[:, t * 32:t * 32 + n], h2_t[u3.par][:, t * P:(t + 1) * P],
                                               wr[u3.layer][:], start=True, stop=True)
                            mm.then_inc(rt_mm, 1)

        @block.vector
        def _(dve):
            def fill(stack, value):
                pair = np.array([(value << 16) | value], np.uint32).view(np.float32)[0]
                for r in (32, 96):
                    last = dve.memset(stack[r:r + 32].bitcast(F32), float(pair))
                return last

            ONE, MINUS_ONE = 0x3F80, 0xBF80
            dve.memset(ident[:], 0.0).then_inc(dve_const, 1)
            dve.memset(neg_half[:], -0.5)
            dve.memset(ones_b[:], 1.0)
            dve.memset(ones_row[:], 1.0)
            fill(k_stk[0][0], MINUS_ONE)
            fill(k_stk[0][1], MINUS_ONE).then_inc(dve_const, 1)
            fill(q_stk[0], ONE)
            fill(q_stk[1], ONE).then_inc(dve_const, 1)
            dve.wait_ge(pool_const, 2)
            dve.tensor_copy(ident_b[:], ident[:]).then_inc(dve_const, 1)
            dve.wait_ge(first_loaded, 16 * FIRST_LOADS)

            def split(src, rest, part, done, c):
                dve.tensor_copy(part[:, 0], src).then_inc(done, 1)
                dve.wait_ge(done, c + 1)
                dve.tensor_tensor(rest[:, 0], src, part[:, 0], ALU.subtract).then_inc(done, 1)
                dve.wait_ge(done, c + 2)
                dve.tensor_copy(part[:, 1], rest[:, 0]).then_inc(done, 1)
                dve.wait_ge(done, c + 3)
                dve.tensor_tensor(rest[:, 1], rest[:, 0], part[:, 1], ALU.subtract).then_inc(done, 1)
                dve.wait_ge(done, c + 4)
                dve.tensor_copy(part[:, 2], rest[:, 1]).then_inc(done, 1)

            def silu(l):
                dve.wait_ge(c_tanh, 1 + 2 * l)
                dve.scalar_tensor_tensor(out=c_si2[l][:], in0=c_th[l][:], scalar=1.0, in1=c_t[l][:], op0=ALU.add,
                                         op1=ALU.mult).then_inc(c_silu, 1)
                dve.wait_ge(c_silu, 2 * l + 1)
                dve.tensor_scalar(c_si[l][:], c_si2[l][:], 0.5, None, ALU.mult).then_inc(c_silu, 1)

            def modulation(l):
                dve.wait_ge(mod_mm, l + 1)
                m = ps_g[:, 0:4 * B].rearrange("p (a b) -> p a b", b=B)
                for i in range(2):
                    dve.tensor_scalar(mod[l][:, i::2, :], m[:, i::2, :], float(i), None, ALU.add).then_inc(mod_ok, 1)
                g = ps_u[0:B, 0:2 * D]
                dve.tensor_scalar(g_up[l], g, 0.25, None, ALU.max).then_inc(gate_ok, 1)
                dve.tensor_scalar(g_down[l], g, -0.25, None, ALU.min).then_inc(gate_ok, 1)
                dve.wait_ge(gate_ok, GATE_STEPS * l + 2)
                dve.scalar_tensor_tensor(out=g_pos[l], in0=g, scalar=0.0, in1=g_up[l], op0=ALU.is_ge,
                                         op1=ALU.mult).then_inc(gate_ok, 1)
                dve.scalar_tensor_tensor(out=g_neg[l], in0=g, scalar=0.0, in1=g_down[l], op0=ALU.is_lt,
                                         op1=ALU.mult).then_inc(gate_ok, 1)
                dve.wait_ge(gate_ok, GATE_STEPS * l + 4)
                dve.tensor_tensor(g_row[l][:], g_pos[l], g_neg[l], ALU.add).then_inc(gate_ok, 1)

            silu(0)
            dve.tensor_scalar(ali[:], pos[:], slopes[:], None, ALU.mult).then_inc(ali_ok, 1)
            dve.wait_ge(ali_ok, 1)
            split(ali[:], ali_rest, ali_part, ali_ok, 1)
            modulation(0)

            def second_setup():
                for k in k_stk[1]:
                    fill(k, MINUS_ONE)
                for v in v_ext:
                    dve.memset(v[:, :, :, DH + 1:VW], 0.0)
                    dve.memset(v[:, :, :, DH:DH + 1], 1.0)
                dve.memset(b_stack[:], 0.0)
                dve.wait_ge(rest_loaded, 16 * REST_LOADS)
                dve.tensor_scalar(bd2[:], bd[:], 2.0, None, ALU.mult).then_inc(dve_const, 1)
                dve.tensor_scalar(b_in[:, 1, :], b_in[:, 1, :], 1.0, None, ALU.add).then_inc(bias_ok, 1)
                dve.wait_ge(bias_ok, 1)
                split(b_in[:].rearrange("e g f -> e (g f)"), b_rest, b_part, bias_ok, 1)
                silu(1)
                modulation(1)
                dve.wait_ge(bov_mm, 1)
                dve.tensor_tensor(bo_v[:], ps_o[0:1, 0:D], bo[:], ALU.add).then_inc(bov_ok, 1)

            def norm_stats(u, i, t):
                dve.bn_stats(ln_st[i][:, t, :], x[:, bass.ds(u.batch, 1), t, :].rearrange("p b d -> p (b d)"))\
                   .then_inc(ln_done[i], 1)

            def norm_mean(u, i):
                ready = apart(dve, pool_const, u.count(6, 2))
                dve.wait_ge(ln_done[i], ready)
                for t in range(TT):
                    dve.bn_aggr(ln_mv[i][:, t, :], ln_st[i][:, t, :]).then_inc(ln_done[i], 1)

            def norm_apply(u, i, used):
                dve.wait_ge(ln_rstd[i], u.count(2, 2))
                if u.has(1):
                    dve.wait_ge(used, u.count(1, 0))
                for t in range(TT):
                    dve.tensor_scalar(xn[i][:, t:t + 1, :], x[:, bass.ds(u.batch, 1), t, :], ln_mv[i][:, t, 0:1],
                                      ln_rs[i][:, t:t + 1], ALU.subtract, ALU.mult).then_inc(ln_done[i], 1)

            def max_split(u, half, step):
                c = 4 * half
                src, rest, part = mx[:, half], mx_rest[:, half], mx_part[half]
                if step == 0:
                    dve.wait_ge(max_done, u.count(16, 8 * half + 8))
                    if u.has(1):
                        dve.wait_ge(mxt_mm, u.count(2, half - 1))
                    dve.tensor_copy(part[:, :, 0, :], src).then_inc(mx_split, 1)
                if step == 1:
                    dve.wait_ge(mx_split, u.count(8, c + 1))
                    dve.tensor_tensor(rest, src, part[:, :, 0, :], ALU.subtract).then_inc(mx_split, 1)
                if step == 2:
                    dve.wait_ge(mx_split, u.count(8, c + 2))
                    dve.tensor_copy(part[:, :, 1, :], rest).then_inc(mx_split, 1)
                if step == 3:
                    dve.wait_ge(mx_split, u.count(8, c + 3))
                    dve.tensor_tensor(part[:, :, 2, :], rest, part[:, :, 1, :], ALU.subtract).then_inc(mx_split, 1)

            def clip_gate(u, q):
                if u.layer == 0:
                    dve.wait_ge(g_mm, u.count(4, q + 1))
                    if u.has(1) or q:
                        dve.wait_ge(th_ok, u.count(4, q))
                    dve.tensor_scalar(g_sb[:], ps_g[:], LIMIT, None, ALU.min).then_inc(g_clip, 1)

            def clip_up(u, q):
                if u.layer == 0:
                    dve.wait_ge(u_mm, u.count(4, q + 1))
                    if u.has(1) or q:
                        dve.wait_ge(uw_ok, u.count(4, q))
                    dve.tensor_scalar(u_sb[:], ps_u[:], 1.0 - LIMIT, 1.0 + LIMIT, ALU.max, ALU.min).then_inc(u_taken, 1)

            def glu(u, q):
                dve.wait_ge(th_ok, u.count(4, q + 1))
                if u.has(1) or q >= 2:
                    dve.wait_ge(actw_ok, u.count(4, q - 1))
                dve.scalar_tensor_tensor(out=glu_sb[q % 2][:], in0=th_sb[:], scalar=1.0,
                                         in1=g_sb[:] if u.layer == 0 else ps_g[:], op0=ALU.add, op1=ALU.mult)\
                   .then_inc(glu_ok, 1)

            def shared_act(u, t):
                if u.layer == 1:
                    dve.wait_ge(sh_th_ok, u.count1(2, t + 1))
                    dve.scalar_tensor_tensor(out=sh_glu[:], in0=sh_th[:], scalar=1.0, in1=ps_g[:, 0:FS], op0=ALU.add,
                                             op1=ALU.mult).then_inc(sh_glu_ok, 1)
                    dve.wait_ge(sh_glu_ok, u.count1(2, t + 1))
                    dve.wait_ge(sg_ok, u.count1(1, 1))
                    if u.first > B or t:
                        dve.wait_ge(sht_mm, u.count1(2, t))
                    dve.scalar_tensor_tensor(out=sh_act[:], in0=sh_glu[:], scalar=sh_gate[:, t:t + 1],
                                             in1=ps_g[:, FS:2 * FS], op0=ALU.mult, op1=ALU.mult).then_inc(sh_act_ok, 1)

            def normalise(u, t):
                dve.wait_ge(ot_mm, u.count(2, t + 1))
                o = ps_job[BANK[f"o_t{t}"]][:].rearrange("p (h v) -> p h v", v=VW)
                dve.reciprocal(den_r[:, t, :].rearrange("p (h o) -> p h o", o=1), o[:, :, DH:DH + 1]).then_inc(ctx_norm, 1)
                dve.wait_ge(ctx_norm, u.count(4, 2 * t + 1))
                if t == 0 and u.has(1):
                    dve.wait_ge(ctx_mm, u.count(1, 0))
                dve.tensor_tensor(ctx_sb[:, t, :].rearrange("p (h d) -> p h d", d=DH), o[:, :, 0:DH],
                                  den_r[:, t, :].rearrange("p (h o) -> p h o", o=1).broadcast_to([P, H, DH]), ALU.mult)\
                   .then_inc(ctx_norm, 1)

            def scale_ffn(u, t):
                dve.wait_ge(dn_mm, u.count(2, t + 1))
                dve.wait_ge(gate_b_in[u.par], u.count_pair(16))
                if u.has(1):
                    dve.wait_ge(ffn_added, u.count(2, t - 1))
                dve.tensor_tensor(ffn_tmp[:, t, :], ps_job[BANK[f"down{t}"]][:, 0:D], gate_b[u.par][:], ALU.mult)\
                   .then_inc(ffn_scaled, 1)

            def top_two(u, step):
                n = E + u.layer
                if step == 0:
                    dve.wait_ge(rt_mm, u.count(1, 1))
                    r = ps_job[BANK["router"]][:, 0:TT * 32].rearrange("p (t e) -> p t e", e=32)
                    dve.tensor_copy(lg[:, :, 0:n], r[:, :, 0:n]).then_inc(top_step, 1)
                if step == 1:
                    ready = apart(dve, pool_const, u.count(9, 1))
                    dve.wait_ge(top_step, ready)
                    for t in range(TT):
                        dve.max(top8[:, t, :], lg[:, t, 0:E]).then_inc(top_step, 1)
                    if u.layer == 1:
                        dve.tensor_copy(dz[:, 1, :], lg[:, :, E]).then_inc(z_ok, 1)
                if step == 2:
                    ready = apart(dve, pool_const, u.count(9, 3))
                    dve.wait_ge(top_step, ready)
                    for t in range(TT):
                        dve.max_index(idx8[:, t, :], top8[:, t, :], lg[:, t, 0:E]).then_inc(top_step, 1)
                if step == 3:
                    dve.wait_ge(top_step, u.count(9, 5))
                    if u.has(1):
                        dve.wait_ge(score_step, u.count(5, -1))
                    dve.tensor_copy(idx_f[:], idx8[:, :, 0:2]).then_inc(top_step, 1)
                    dve.tensor_tensor(dz[:, 0, :], top8[:, :, 0], top8[:, :, 1], ALU.subtract).then_inc(top_step, 1)

            def top_weights(u):
                dve.wait_ge(top_tanh, u.count(1, 1))
                for k, sign in ((0, 0.25), (1, -0.25)):
                    dve.tensor_scalar(w_top[:, k, :], dz_th[:, 0, :], sign, 0.25, ALU.mult, ALU.add).then_inc(top_step, 1)
                if u.layer == 1:
                    dve.tensor_scalar(sh_gate[:], dz_th[:, 1, :], 0.25, 0.25, ALU.mult, ALU.add).then_inc(sg_ok, 1)

            for u0, u1, u2, u3, u4, u5 in iterations(dve):
                if u0.first == 1:
                    second_setup()
                if u0.first == 0:
                    dve.wait_ge(x_first, 16 * TT)
                if u0.first == LAGS - 1:
                    dve.wait_ge(x_rest, 16 * TT)
                for k in range(H):
                    if u1.live:
                        dve.wait_ge(s_mm, u1.count(16, k + 1))
                        hp, par = k // 2, k % 2
                        dve.tensor_reduce(mx[:, hp // 4, :, 4 * par + hp % 4],
                                          ps_s[:].rearrange("p (t s) -> p t s", s=S), AX_X, ALU.max).then_inc(max_done, 1)
                    if k == 0:
                        if u0.live and u0.layer == 1:
                            dve.wait_ge(ffn_added, u0.count(2, 2 - 2 * B))
                        for step in range(4):
                            if u2.live:
                                max_split(u2, 1, step)
                            if u0.live and step < TT:
                                norm_stats(u0, 0, step)
                        if u0.live:
                            norm_mean(u0, 0)
                    if k == 2 and u0.live:
                        norm_apply(u0, 0, h_mm)
                    if k == 5 and u3.live:
                        normalise(u3, 0)
                    if k == 6 and u3.live:
                        normalise(u3, 1)
                    if k == 1 and u4.live:
                        top_two(u4, 0)
                    if k == 2 and u4.live:
                        top_two(u4, 2)
                    if u4.live:
                        for q in range(NQ):
                            if k == GATE_STEP[u4.layer][q] + 1:
                                clip_gate(u4, q)
                            if k == GATE_STEP[u4.layer][q] + 2 - u4.layer:
                                glu(u4, q)
                            if k == UP_STEP[q] + 1:
                                clip_up(u4, q)
                        for t in range(TT):
                            if k == SHARED_STEP[t] + 1:
                                shared_act(u4, t)
                    if k == 1 and u4.live:
                        top_two(u4, 1)
                    if k == 2 and u4.live:
                        top_two(u4, 3)
                    if k == 3 and u4.live:
                        top_weights(u4)
                    if k == 7 and u5.live:
                        scale_ffn(u5, 1)
                    if k == 8 and u1.live:
                        for step in range(4):
                            max_split(u1, 0, step)
                    if k == 9 and u3.live:
                        dve.wait_ge(wo_mm, u3.count(1, 1))
                        dve.wait_ge(gate_a_in[u3.par], u3.count_pair(16))
                        if u3.has(1):
                            dve.wait_ge(att_added, u3.count(1, 0))
                        dve.tensor_tensor(att_tmp[:], ps_job[BANK["wo"]][:, 0:TT * D].rearrange("p (t d) -> p t d", d=D),
                                          gate_a[u3.par][:].rearrange("p (o d) -> p o d", o=1).broadcast_to([P, TT, D]),
                                          ALU.mult).then_inc(att_scaled, 1)
                    if k == 10 and u3.live:
                        dve.wait_ge(att_added, u3.count(1, 1))
                        for t in range(TT):
                            norm_stats(u3, 1, t)
                        norm_mean(u3, 1)
                    if k == 12 and u3.live:
                        norm_apply(u3, 1, h2_mm)
                    if k == 13 and u4.live:
                        scale_ffn(u4, 0)
                    if k == 15 and u3.live:
                        dve.wait_ge(h2_rounded, u3.count(1, 1))
                        dve.tensor_tensor(h2_lo[u3.par][:], h2_t[u3.par][:], h2_hi[u3.par][:], ALU.subtract)\
                           .then_inc(h2_rest, 1)


def kernel(**inputs):
    import concourse.bacc as bacc
    from concourse.bass_utils import run_bass_kernel_spmd

    a = {n: np.ascontiguousarray(v) for n, v in inputs.items()}
    gu0 = a["L0_ffn_gate_up_proj"].reshape(E, D, F, 2).transpose(1, 3, 0, 2).reshape(D, 2, E * F)
    heads = lambda w: w.transpose(1, 0, 2).reshape(D, D)
    arrays = {
        "x": a["L0_attn_x"],
        "c0": a["L0_c"].T, "c1": a["L1_c"].T, "wmod0": a["L0_wmod"], "wmod1": a["L1_wmod"],
        "wq0": a["L0_attn_Wq"].T, "wk0": a["L0_attn_Wk"].T, "wv0": a["L0_attn_Wv"].T, "wo0": a["L0_attn_Wo"].T,
        "bq": a["L0_attn_bq"].reshape(D, 1), "bk": a["L0_attn_bk"].reshape(D, 1), "bv": a["L0_attn_bv"].reshape(D, 1),
        "bo": a["L0_attn_bo"].reshape(1, D), "slopes": a["L0_attn_slopes"].reshape(H, 1),
        "wr0": a["L0_ffn_router_weight"], "wgu0": gu0,
        "b_gu": a["L0_ffn_gate_up_proj_bias"].reshape(E, F, 2).transpose(0, 2, 1),
        "wd0": a["L0_ffn_down_proj"].reshape(E // 2, 2 * F, D).transpose(1, 0, 2), "bd": a["L0_ffn_down_proj_bias"],
        "wq1": heads(a["L1_attn_W_query"]), "wk1": heads(a["L1_attn_W_key"]), "wv1": heads(a["L1_attn_W_val"]),
        "wo1": a["L1_attn_W_out"].reshape(D, D), "wr1": a["L1_ffn_router_w"].T, "wsg": a["L1_ffn_shared_gate_w"],
        "wgu1": np.stack([a["L1_ffn_Wg"].transpose(1, 0, 2).reshape(D, E * F),
                          a["L1_ffn_Wu"].transpose(1, 0, 2).reshape(D, E * F)], axis=1),
        "wd1": a["L1_ffn_Wd"].reshape(E // 2, 2 * F, D).transpose(1, 0, 2),
        "wsgu": np.stack([a["L1_ffn_Sg"], a["L1_ffn_Su"]], axis=1),
        "wsd": a["L1_ffn_Sd"].reshape(FS // P, P, D).transpose(1, 0, 2),
    }
    nc = bacc.Bacc("TRN2", target_bir_lowering=False, num_devices=1)
    feeds, io = {}, {}
    for name, v in arrays.items():
        v = np.ascontiguousarray(v)
        feeds[f"in_{name}"] = v
        io[name] = nc.dram_tensor(f"in_{name}", v.shape, mybir.dt.from_np(v.dtype), kind="ExternalInput").ap()
    out = nc.dram_tensor("out_x", (B, S, D), F32, kind="ExternalOutput").ap()
    build(nc, io, out)
    r = run_bass_kernel_spmd(nc, [feeds], core_ids=[0])
    return r.results[0]["out_x"]
```
